# Optimizing a Trainium2 kernel written in Bass

```python
import numpy as np
import jax
import jax.numpy as jnp

def _softmax(x, axis=-1):
    return jax.nn.softmax(x, axis=axis)

def _gelu(x):
    return jax.nn.gelu(x, approximate=True)

def _silu(x):
    return jax.nn.silu(x)

def _sigmoid(x):
    return jax.nn.sigmoid(x)

def _layernorm(x, axis=-1, eps=1e-05):
    m = jnp.mean(x, axis=axis, keepdims=True)
    v = jnp.var(x, axis=axis, keepdims=True)
    return (x - m) / jnp.sqrt(v + eps)

def _scatter_add(tgt, idx, src, axis=0):
    return tgt.at[idx].add(src)

def _segment_sum(src, seg, n):
    return jax.ops.segment_sum(src, seg, n)
kernel_name = 'mk_seq_preln_d1_jaxref_r4_6ff3fe'

def setup_inputs(seed: int=0):
    np.random.seed(seed)
    _w = jnp.asarray

    def _L0_attn_setup():
        import jax, jax.numpy as jnp
        import numpy as np
        EMBED_DIM = 256
        NUM_HEADS = 16
        HEAD_DIM = EMBED_DIM // NUM_HEADS
        B, T = (2, 512)
        key = jax.random.key(seed)
        k1, k2, k3 = jax.random.split(key, 3)
        x = jax.random.normal(k1, (B, T, EMBED_DIM), dtype=jnp.float32)
        W_qkv = jax.random.normal(k2, (EMBED_DIM, 3 * EMBED_DIM), dtype=jnp.float32) * (1.0 / np.sqrt(EMBED_DIM))
        b_qkv = jnp.zeros((3 * EMBED_DIM,), dtype=jnp.float32)
        W_out = jax.random.normal(k3, (EMBED_DIM, EMBED_DIM), dtype=jnp.float32) * (1.0 / np.sqrt(EMBED_DIM))
        b_out = jnp.zeros((EMBED_DIM,), dtype=jnp.float32)
        return {'x': x, 'W_qkv': W_qkv, 'b_qkv': b_qkv, 'W_out': W_out, 'b_out': b_out}
    _L0_attn_in = _L0_attn_setup()

    def _L0_ffn_setup():
        import jax, jax.numpy as jnp
        import numpy as np
        D_MODEL = 256
        FF = 1024
        E = 8
        TOP_K = 2
        CAP_FACTOR = 1.25
        B, T = (4, 512)

        def _moe_forward(x, gate_w, gate_b, w1, b1, w2, b2):
            Bb, Tt, d = x.shape
            S = Bb * Tt
            C = int(CAP_FACTOR * S / E)
            xf = x.reshape(S, d)
            logits = xf @ gate_w + gate_b
            probs = jax.nn.softmax(logits, axis=1)
            topk_p, topk_i = jax.lax.top_k(probs, TOP_K)
            topk_pn = topk_p / jnp.sum(topk_p, axis=1, keepdims=True)
            rows = jnp.arange(S)
            w_te = jnp.zeros((S, E), xf.dtype).at[rows[:, None], topk_i].set(topk_pn)
            mask = jnp.zeros((S, E), bool).at[rows[:, None], topk_i].set(True)
            rank = jnp.cumsum(mask.astype(jnp.int32), axis=0)
            slot = jnp.where(mask & (rank <= C), rank - 1, C)
            e_grid = jnp.broadcast_to(jnp.arange(E), (S, E))
            t_grid = jnp.broadcast_to(rows[:, None], (S, E))
            buf = jnp.full((E, C + 1), S, jnp.int32).at[e_grid, slot].set(t_grid)
            idx = buf[:, :C]
            valid = idx < S
            x_pad = jnp.concatenate([xf, jnp.zeros((1, d), xf.dtype)], axis=0)
            xin = x_pad[idx]
            h = jax.nn.relu(jnp.einsum('ecd,edh->ech', xin, w1) + b1[:, None, :])
            out = jnp.einsum('ech,ehd->ecd', h, w2) + b2[:, None, :]
            w_pad = jnp.concatenate([w_te, jnp.zeros((1, E), xf.dtype)], axis=0)
            tok_w = w_pad[idx, jnp.arange(E)[:, None]]
            out = out * jnp.where(valid, tok_w, 0.0)[:, :, None]
            final = jnp.zeros((S + 1, d), xf.dtype).at[idx.reshape(-1)].add(out.reshape(-1, d))[:S]
            return final.reshape(Bb, Tt, d)
        key = jax.random.key(seed)
        ks = jax.random.split(key, 7)
        s = 0.02
        return {'x': jax.random.normal(ks[0], (B, T, D_MODEL), jnp.float32), 'gate_w': jax.random.normal(ks[1], (D_MODEL, E), jnp.float32) * s, 'gate_b': jnp.zeros((E,), jnp.float32), 'w1': jax.random.normal(ks[2], (E, D_MODEL, FF), jnp.float32) * s, 'b1': jnp.zeros((E, FF), jnp.float32), 'w2': jax.random.normal(ks[3], (E, FF, D_MODEL), jnp.float32) * s, 'b2': jnp.zeros((E, D_MODEL), jnp.float32)}
    _L0_ffn_in = _L0_ffn_setup()
    _d = {'L0_attn_x': _L0_attn_in['x'], 'L0_attn_W_qkv': _L0_attn_in['W_qkv'], 'L0_attn_b_qkv': _L0_attn_in['b_qkv'], 'L0_attn_W_out': _L0_attn_in['W_out'], 'L0_attn_b_out': _L0_attn_in['b_out'], 'L0_ffn_gate_w': _L0_ffn_in['gate_w'], 'L0_ffn_gate_b': _L0_ffn_in['gate_b'], 'L0_ffn_w1': _L0_ffn_in['w1'], 'L0_ffn_b1': _L0_ffn_in['b1'], 'L0_ffn_w2': _L0_ffn_in['w2'], 'L0_ffn_b2': _L0_ffn_in['b2']}
    _x0 = _d['L0_attn_x']
    _d['L0_attn_x'] = jax.random.normal(jax.random.fold_in(jax.random.key(seed), 1), (1, 4096, 256), dtype=_x0.dtype)
    del _x0
    return _d

def reference(L0_attn_x, L0_attn_W_qkv, L0_attn_b_qkv, L0_attn_W_out, L0_attn_b_out, L0_ffn_gate_w, L0_ffn_gate_b, L0_ffn_w1, L0_ffn_b1, L0_ffn_w2, L0_ffn_b2):

    def _L0_attn_ref(x, W_qkv, b_qkv, W_out, b_out):
        import jax, jax.numpy as jnp
        import numpy as np
        EMBED_DIM = 256
        NUM_HEADS = 16
        HEAD_DIM = EMBED_DIM // NUM_HEADS
        B, T = (2, 512)
        Bc, Tc, E = x.shape
        H, D = (NUM_HEADS, HEAD_DIM)
        qkv = (x @ W_qkv + b_qkv).reshape(Bc, Tc, 3, H, D)
        q, k, v = jnp.transpose(qkv, (2, 0, 3, 1, 4))
        scores = jnp.einsum('bhqd,bhkd->bhqk', q, k) / jnp.sqrt(jnp.float32(D))
        attn = jax.nn.softmax(scores, axis=-1)
        out = jnp.einsum('bhqk,bhkd->bhqd', attn, v)
        out = out.reshape(Bc, Tc, E)
        return out @ W_out + b_out

    def _L0_ffn_ref(x, gate_w, gate_b, w1, b1, w2, b2):
        import jax, jax.numpy as jnp
        import numpy as np
        D_MODEL = 256
        FF = 1024
        E = 8
        TOP_K = 2
        CAP_FACTOR = 1.25
        B, T = (4, 512)

        def _moe_forward(x, gate_w, gate_b, w1, b1, w2, b2):
            Bb, Tt, d = x.shape
            S = Bb * Tt
            C = int(CAP_FACTOR * S / E)
            xf = x.reshape(S, d)
            logits = xf @ gate_w + gate_b
            probs = jax.nn.softmax(logits, axis=1)
            topk_p, topk_i = jax.lax.top_k(probs, TOP_K)
            topk_pn = topk_p / jnp.sum(topk_p, axis=1, keepdims=True)
            rows = jnp.arange(S)
            w_te = jnp.zeros((S, E), xf.dtype).at[rows[:, None], topk_i].set(topk_pn)
            mask = jnp.zeros((S, E), bool).at[rows[:, None], topk_i].set(True)
            rank = jnp.cumsum(mask.astype(jnp.int32), axis=0)
            slot = jnp.where(mask & (rank <= C), rank - 1, C)
            e_grid = jnp.broadcast_to(jnp.arange(E), (S, E))
            t_grid = jnp.broadcast_to(rows[:, None], (S, E))
            buf = jnp.full((E, C + 1), S, jnp.int32).at[e_grid, slot].set(t_grid)
            idx = buf[:, :C]
            valid = idx < S
            x_pad = jnp.concatenate([xf, jnp.zeros((1, d), xf.dtype)], axis=0)
            xin = x_pad[idx]
            h = jax.nn.relu(jnp.einsum('ecd,edh->ech', xin, w1) + b1[:, None, :])
            out = jnp.einsum('ech,ehd->ecd', h, w2) + b2[:, None, :]
            w_pad = jnp.concatenate([w_te, jnp.zeros((1, E), xf.dtype)], axis=0)
            tok_w = w_pad[idx, jnp.arange(E)[:, None]]
            out = out * jnp.where(valid, tok_w, 0.0)[:, :, None]
            final = jnp.zeros((S + 1, d), xf.dtype).at[idx.reshape(-1)].add(out.reshape(-1, d))[:S]
            return final.reshape(Bb, Tt, d)
        return _moe_forward(x, gate_w, gate_b, w1, b1, w2, b2)
    x = L0_attn_x
    x = x + _L0_attn_ref(_layernorm(x, axis=-1), L0_attn_W_qkv, L0_attn_b_qkv, L0_attn_W_out, L0_attn_b_out)
    x = x + _L0_ffn_ref(_layernorm(x, axis=-1), L0_ffn_gate_w, L0_ffn_gate_b, L0_ffn_w1, L0_ffn_b1, L0_ffn_w2, L0_ffn_b2)
    return x

_drawn_inputs = setup_inputs


def setup_inputs(seed=0):
    import zlib

    import numpy as np

    out = dict(_drawn_inputs(seed))
    spreads = {'L0_attn_b_qkv': (0.0, 0.1),
     'L0_attn_b_out': (0.0, 0.1),
     'L0_ffn_gate_b': (0.0, 0.1),
     'L0_ffn_b1': (0.0, 0.323),
     'L0_ffn_b2': (0.0, 0.1)}
    factors = {}
    for name, (base, spread) in spreads.items():
        noise = np.random.default_rng([zlib.crc32(name.encode()), seed]).standard_normal(out[name].shape)
        drawn = base * np.exp(spread * noise) if base else spread * noise
        out[name] = jnp.asarray(drawn.astype(out[name].dtype))
    for name, factor in factors.items():
        out[name] = (out[name] * factor).astype(out[name].dtype)
    return out
```

```python
from contextlib import ExitStack

import numpy as np

import concourse.bass as bass
from concourse import mybir

F32 = mybir.dt.float32
BF16 = mybir.dt.bfloat16
U32 = mybir.dt.uint32
ALU = mybir.AluOpType
ACT = mybir.ActivationFunctionType
AX = mybir.AxisListType
ds = bass.ds

P = 128
T, D, H, HD = 4096, 256, 16, 16
NT = T // P
QW = 512
NQ = T // QW
TPB = QW // P
STEPS = H * NQ
NCH = T // QW
E, FF = 8, 1024
CAP = int(1.25 * T / E)
ST = CAP // P
KC = D // P
FT = FF // P
EPS = 1e-5
SCALE = 1.0 / float(np.sqrt(HD))
Q_PARTS = (0, 1, 2, 0, 1, 0)
K_PARTS = (0, 0, 0, 1, 1, 2)
NPR = 16 * len(Q_PARTS)
NAUG = NPR + 3
QRING, KRING = 16, 24
Q_AHEAD, K_AHEAD = 4, 12
VW = 32
EXPS = T // P
UNITS = TPB * NCH
RING = 3
GROUPS = T // (4 * P)
PV_LAG = 2
BIG = 1.0e6
CW = P + P + 32 + E + E


def freed(n):
    assert EXPS % RING == 2 and UNITS % RING == 2
    return n + 1 if n >= 2 else n + 2


class Chain:

    def __init__(self, eng, sem, base=0):
        self.eng, self.sem, self.n = eng, sem, base

    def __call__(self, ins):
        ins.then_inc(self.sem, 1)
        self.n = self.n + 1
        self.eng.wait_ge(self.sem, self.n)


def build(nc, x, w_qkv, b_qkv, w_out, b_out, gate_w, gate_b, w1, b1, w2, b2, consts, out):
    qk_d = nc.dram_tensor("qk_parts", (2, 3, D, T), BF16, kind="Internal").ap()
    v_d = nc.dram_tensor("v_heads", (H, P, NT * VW), F32, kind="Internal").ap()
    att_d = nc.dram_tensor("attention_rows", (STEPS * QW, HD), F32, kind="Internal").ap()
    xin_d = nc.dram_tensor("expert_in", (E * CAP, D), F32, kind="Internal").ap()
    y_d = nc.dram_tensor("expert_out", (E * CAP, D), F32, kind="Internal").ap()

    with ExitStack() as ctx:
        def sb(name, cols, dt=F32):
            return ctx.enter_context(nc.sbuf_tensor(name, [P, cols], dt))

        def sem(name):
            return ctx.enter_context(nc.semaphore(name))

        cst = sb("cst", CW)
        ident = cst[:, 0:P]
        fold = cst[:, 2 * P:2 * P + 32]
        iota_e = cst[:, 2 * P + 32:2 * P + 32 + E]
        slot_base = cst[:, 2 * P + 32 + E:CW]
        identb = sb("identb", P, BF16)
        trib = sb("trib", P, BF16)
        onesb = sb("onesb", P, BF16)
        x_all = sb("x_all", NT * D)
        a_all = sb("a_all", NT * D)
        arena = sb("arena", (KRING + QRING) * QW // 2 + 4096)
        extra = sb("extra", 2048)
        wbuf = sb("wbuf", 8192)
        v_sb = sb("v_sb", NT * VW)
        o_sb = sb("o_sb", QW)
        wqkv = sb("wqkv", KC * 3 * D)
        wout = sb("wout", KC * D)
        wgate = sb("wgate", KC * E)
        bqk = sb("bqk", 4)
        bv = sb("bv", D)
        bout = sb("bout", D)
        bgate = sb("bgate", E)
        b1s = sb("b1s", 2 * FT)
        b2s = sb("b2s", 2 * D)
        stats = sb("stats", TPB * 6)
        mv = sb("mv", TPB * 2)
        rstd = sb("rstd", TPB)
        dev = sb("dev", TPB)
        eps = sb("eps", 1)
        mpart = sb("mpart", UNITS)
        mx = sb("mx", TPB)
        mneg = sb("mneg", TPB)
        mres = sb("mres", TPB)
        msplit = sb("msplit", TPB * 4, BF16)
        rden = sb("rden", TPB)
        zeros = sb("zeros", 2 * D)
        rows = sb("rows", 2 * TPB * HD)

        x_t = x_all[:].rearrange("p (t c) -> p t c", t=NT)
        a_t = a_all[:].rearrange("p (t c) -> p t c", t=NT)
        kcols, qcols = KRING * QW // 2, QRING * QW // 2
        k_ring = arena[:, 0:kcols].bitcast(BF16)
        q_ring = arena[:, kcols:kcols + qcols].bitcast(BF16)
        p_ring = arena[:, kcols + qcols:kcols + qcols + 4096].rearrange("p (s c) -> p s c", s=8)
        parts = [arena[:, o:o + 3072].bitcast(BF16).rearrange("p (f n c) -> p f n c", f=4, n=3)
                 for o in (kcols, kcols + 3072)]
        res = arena[:, kcols + 6144:kcols + 7168].rearrange("p (s c) -> p s c", s=2)
        vst = [wbuf[:, o:o + 2048].rearrange("p (h t c) -> p h t c", h=H, t=TPB) for o in (0, 2048)]
        xf = wbuf[:, 4096:6144].rearrange("p (f c) -> p f c", f=4)
        xn = [wbuf[:, 6144:7168].rearrange("p (t c) -> p t c", t=TPB),
              wbuf[:, 7168:8192].rearrange("p (t c) -> p t c", t=TPB)]
        xnT = [extra[:, 1024 * i:1024 * i + 1024].rearrange("p (k c) -> p k c", k=KC) for i in (0, 1)]
        at = [extra[:, 256 * i:256 * i + 256] for i in (0, 1)]
        atT = [extra[:, 512 + 256 * i:768 + 256 * i] for i in (0, 1)]
        xs = [extra[:, 1024 + 256 * i:1280 + 256 * i] for i in (0, 1)]
        xsT = [extra[:, 1536 + 256 * i:1792 + 256 * i] for i in (0, 1)]
        w1s = [wbuf[:, 4096 * i:4096 * i + 2048].rearrange("p (k f) -> p k f", k=KC) for i in (0, 1)]
        w2s = [wbuf[:, 4096 * i + 2048:4096 * i + 4096].rearrange("p (k c) -> p k c", k=FT) for i in (0, 1)]
        xin = [arena[:, 1280 * i:1280 * i + 1280].rearrange("p (s c) -> p s c", s=ST) for i in (0, 1)]
        xinT = [arena[:, 2560 + 1280 * i:3840 + 1280 * i] for i in (0, 1)]
        ys = [arena[:, 5120 + 1280 * i:6400 + 1280 * i].rearrange("p (s c) -> p s c", s=ST) for i in (0, 1)]
        hT = arena[:, 7680:7680 + FT * CAP].rearrange("p (f c) -> p f c", f=FT)
        rt = [arena[:, 256 * i:256 * i + 256].rearrange("p (t e) -> p t e", e=E) for i in range(20)]
        r1 = [arena[:, 5120 + 32 * i:5152 + 32 * i] for i in range(20)]
        maskb = arena[:, 6144:6272].bitcast(BF16)
        wgt = sb("wgt", 2 * NT)
        slot_w = sb("slot_w", 2 * NT, U32)
        slot_r = sb("slot_r", 2 * NT, U32)
        G = 4
        gat = [[arena[:, 1024 + 256 * (2 * i + j):1280 + 256 * (2 * i + j)] for j in (0, 1)] for i in range(G)]

        ps = ctx.enter_context(nc.psum_tensor("ps", [P, 8 * QW], F32))

        def bank(b, n=1):
            return ps[:, b * QW:(b + n) * QW]

        const_in, x_in, w_in, vec_in = sem("const_in"), sem("x_in"), sem("w_in"), sem("vec_in")
        consts_ready, zeros_ready, vst_ready = sem("consts_ready"), sem("zeros_ready"), sem("vst_ready")
        zero_out = sem("zero_out")
        ln_chain, ln_ready = sem("ln_chain"), sem("ln_ready")
        xt_ready, xt_lo, xt_hi = sem("xt_ready"), sem("xt_lo"), sem("xt_hi")
        proj_ready, proj_read, v_ready, v_evac = sem("proj_ready"), sem("proj_read"), sem("v_ready"), sem("v_evac")
        split_v, split_p, chain_v, chain_p = sem("split_v"), sem("split_p"), sem("chain_v"), sem("chain_p")
        parts_out = [sem("parts_out0"), sem("parts_out1")]
        v_out = [sem("v_out0"), sem("v_out1")]
        ring_ones = sem("ring_ones")
        q_in, k_in, va_in, vb_in = sem("q_in"), sem("k_in"), sem("va_in"), sem("vb_in")
        st_ready, exp_done, pv_done = sem("st_ready"), sem("exp_done"), sem("pv_done")
        s_ready, max_done, mx_ready = sem("s_ready"), sem("max_done"), sem("mx_ready")
        split_chain, msplit_ready, mt_ready, mrow_ready = sem("split_chain"), sem("msplit_ready"), sem("mt_ready"), sem("mrow_ready")
        o_evac, comb_ready, rden_ready, comb_done = sem("o_evac"), sem("comb_ready"), sem("rden_ready"), sem("comb_done")
        at_in, at_tr, atT_copied, proj2_ready = [sem("at_in0"), sem("at_in1")], sem("at_tr"), sem("atT_copied"), sem("proj2_ready")
        rows_out = sem("rows_out")
        x2_chain, xs_ready, xs_tr, xsT_copied = sem("x2_chain"), sem("xs_ready"), sem("xs_tr"), sem("xsT_copied")
        gate_ready, gate_read = sem("gate_ready"), sem("gate_read")
        route_chain, exp_in, exp_out, rank_in, rank_out = sem("route_chain"), sem("gexp_in"), sem("gexp_out"), sem("rank_in"), sem("rank_out")
        slots_ready, scattered = sem("slots_ready"), sem("scattered")
        we_in = [sem("we_in0"), sem("we_in1")]
        xin_in = [sem("xin_in0"), sem("xin_in1")]
        xi_tr, xi_lo, xi_mid, xi_hi = sem("xi_tr"), sem("xi_lo"), sem("xi_mid"), sem("xi_hi")
        h_ready, h_act, h_dve = sem("h_ready"), sem("h_act"), sem("h_dve")
        y_ready, y_read, y_out = sem("y_ready"), sem("y_read"), [sem("y_out0"), sem("y_out1")]
        g_in = [sem(f"g_in{i}") for i in range(G)]
        o_chain, o_ready, out_done = sem("o_chain"), sem("o_ready"), sem("out_done")

        def lone_wait(eng):
            eng.sem_inc(waits_met, 1)

        def chain(eng, done, base):
            link = Chain(eng, done, base)

            def step(ins):
                link(ins)
                lone_wait(eng)
            return step

        var_ready, waits_met = sem("var_ready"), sem("waits_met")
        rstd_ready, dev_ready = sem("rstd_ready"), sem("dev_ready")
        block = ctx.enter_context(nc.Block())

        @block.sync
        def _(sp):
            for par in (0, 1):
                sp.sem_inc(parts_out[par], 12 * 16)
                sp.sem_inc(v_out[par], 16)
                sp.sem_inc(y_out[par], 16)
                sp.sem_inc(rows_out, 16)
            sp.dma_start(cst[:], consts).then_inc(const_in, 16)
            x_tiles = x[0].rearrange("(b t p) c -> b p t c", t=TPB, p=P)
            for b in range(NQ):
                sp.dma_start(x_t[:, TPB * b:TPB * b + TPB, :], x_tiles[b]).then_inc(x_in, 16)
                if b == 0:
                    sp.dma_start(wqkv[:].rearrange("p (k c) -> p k c", k=KC),
                                 w_qkv.rearrange("(k p) c -> p k c", p=P)).then_inc(w_in, 16)
                    sp.dma_start(bqk[:], b_qkv[0:2 * D].rearrange("(f p) -> p f", p=P), allow_slow_non_contiguous=True).then_inc(w_in, 16)
                    sp.dma_start(bv[:], b_qkv[2 * D:3 * D].partition_broadcast(P)).then_inc(w_in, 16)
                sp.wait_ge(x_in, 16 * (b + 1))
            sp.dma_start(wout[:].rearrange("p (k c) -> p k c", k=KC),
                         w_out.rearrange("(k p) c -> p k c", p=P)).then_inc(vec_in, 16)
            sp.dma_start(wgate[:].rearrange("p (k c) -> p k c", k=KC),
                         gate_w.rearrange("(k p) c -> p k c", p=P)).then_inc(vec_in, 16)
            sp.dma_start(bout[:], b_out.partition_broadcast(P)).then_inc(vec_in, 16)
            sp.dma_start(bgate[:], gate_b.partition_broadcast(P)).then_inc(vec_in, 16)
            sp.wait_ge(zeros_ready, 1)
            for i in range(E * CAP // (2 * P)):
                sp.dma_start(xin_d[2 * P * i:2 * P * i + 2 * P, :].rearrange("(p r) c -> p (r c)", r=2),
                             zeros[:]).then_inc(zero_out, 16)

            def store_chunk(c, par):
                for f in range(4):
                    if f < 2:
                        sp.wait_ge(split_v, 2 * c + f + 3)
                    else:
                        sp.wait_ge(split_p, 2 * c + f + 1)
                    for n in range(3):
                        sp.dma_start(qk_d[f // 2, n, (f % 2) * P:(f % 2) * P + P, ds(c * QW, QW)],
                                     parts[par][:, f, n, :]).then_inc(parts_out[par], 16)
                sp.wait_ge(v_evac, 2 * c + 4)
                sp.dma_start(v_d[:, :, ds(c * TPB * VW, TPB * VW)].rearrange("h p c -> p h c"),
                             vst[par].rearrange("p h t c -> p h (t c)")).then_inc(v_out[par], 16)

            with sp.Fori(0, NQ // 2) as i:
                for par in (0, 1):
                    store_chunk(i * 2 + par, par)

            def load_q(j):
                for b, part in enumerate(Q_PARTS):
                    sp.dma_start(q_ring[16 * b:16 * b + 16, ds((j % QRING) * QW, QW)],
                                 qk_d[0, part, ds(((j >> 3) % H) * HD, HD), ds((j % NQ) * QW, QW)]).then_inc(q_in, 16)

            def load_k(j):
                for b, part in enumerate(K_PARTS):
                    sp.dma_start(k_ring[16 * b:16 * b + 16, ds((j % KRING) * QW, QW)],
                                 qk_d[1, part, ds(((j >> 3) % H) * HD, HD), ds((j % NQ) * QW, QW)]).then_inc(k_in, 16)

            half = NT * VW // 2

            def load_v(head, second, done):
                o = half if second else 0
                sp.dma_start(v_sb[:, o:o + half], v_d[ds(head, 1), :, o:o + half].rearrange("h p c -> (h p) c")).then_inc(done, 16)

            for par in (0, 1):
                sp.wait_ge(parts_out[par], 12 * 16 * (NQ // 2 + 1))
                sp.wait_ge(v_out[par], 16 * (NQ // 2 + 1))
            sp.sem_inc(k_in, 96 * (NQ - 1))
            sp.sem_inc(q_in, 96 * (Q_AHEAD - 1))
            for b, part in enumerate(K_PARTS):
                sp.dma_start(k_ring[16 * b:16 * b + 16, 0:T], qk_d[1, part, 0:HD, :]).then_inc(k_in, 16)
            for b, part in enumerate(Q_PARTS):
                sp.dma_start(q_ring[16 * b:16 * b + 16, 0:Q_AHEAD * QW],
                             qk_d[0, part, 0:HD, 0:Q_AHEAD * QW]).then_inc(q_in, 16)
            for j in range(NQ, K_AHEAD):
                load_k(j)
            load_v(0, False, va_in)

            def store_rows(it):
                sp.wait_ge(comb_done, it + 1)
                lone_wait(sp)
                sp.wait_ge(rows_out, 16 * (it + 2))
                sp.dma_start(att_d[ds(it * QW, QW), :].rearrange("(t p) c -> p t c", p=P),
                             rows[:, ds((it % 2) * TPB * HD, TPB * HD)].rearrange("p (t c) -> p t c", c=HD)
                             ).then_inc(rows_out, 16)

            def attention_loads(it):
                sp.wait_ge(q_in, 96 * (it + Q_AHEAD))
                lone_wait(sp)
                sp.wait_ge(k_in, 96 * (it + K_AHEAD))
                lone_wait(sp)
                if not isinstance(it, int) or it > 0:
                    sp.wait_ge(st_ready, EXPS * it)
                    lone_wait(sp)
                load_q(it + Q_AHEAD)
                load_k(it + K_AHEAD)
                sp.wait_ge(pv_done, GROUPS * it + 2)
                load_v((it >> 3) % H, True, vb_in)
                sp.wait_ge(pv_done, GROUPS * it + GROUPS // 2 + 2)
                load_v(((it + 1) >> 3) % H, False, va_in)
                if not isinstance(it, int) or it > 0:
                    store_rows(it - 1)

            def load_expert(e, par):
                sp.dma_start(w1s[par], w1[ds(e, 1)].rearrange("e (k p) f -> p (e k) f", p=P)).then_inc(we_in[par], 16)
                sp.dma_start(w2s[par], w2[ds(e, 1)].rearrange("e (k p) c -> p (e k) c", p=P)).then_inc(we_in[par], 16)
                sp.dma_start(b1s[:, FT * par:FT * par + FT],
                             b1[ds(e, 1)].rearrange("e (f p) -> p (e f)", p=P), allow_slow_non_contiguous=True).then_inc(we_in[par], 16)
                sp.dma_start(b2s[:, D * par:D * par + D],
                             b2[ds(e, 1)].rearrange("e c -> (e c)").partition_broadcast(P)).then_inc(we_in[par], 16)

            load_expert(0, 0)
            load_expert(1, 1)
            attention_loads(0)
            with sp.Fori(1, STEPS) as it:
                attention_loads(it)
            store_rows(STEPS - 1)
            sp.wait_ge(q_in, 96 * (STEPS + Q_AHEAD))
            sp.wait_ge(k_in, 96 * (STEPS + K_AHEAD))
            sp.wait_ge(va_in, 16 * (STEPS + 1))
            sp.wait_ge(rows_out, 16 * (STEPS + 2))

            def load_rows(t, i, par):
                sp.wait_ge(at_tr, t + 1)
                sp.dma_start(at[par], att_d[ds(t * P * D // HD, P * D // HD), :].rearrange("(p k) c -> p (k c)", p=P)
                             ).then_inc(at_in[par], 16)

            with sp.Fori(0, NT // 2) as i:
                for par in (0, 1):
                    load_rows(i * 2 + par, i, par)

            def load_slots(e, par):
                sp.dma_start(xin[par], xin_d[ds(e * CAP, CAP), :].rearrange("(s p) c -> p s c", p=P)).then_inc(xin_in[par], 16)

            sp.wait_ge(scattered, 16 * 2 * NT)
            load_slots(0, 0)
            load_slots(1, 1)

            def expert_io(e, par, more):
                sp.wait_ge(y_read, ST * (e + 1) + 2)
                sp.dma_start(y_d[ds(e * CAP, CAP), :].rearrange("(s p) c -> p s c", p=P), ys[par]).then_inc(y_out[par], 16)
                if more:
                    load_expert(e + 2, par)
                    load_slots(e + 2, par)

            with sp.Fori(0, E // 2 - 1) as i:
                for par in (0, 1):
                    expert_io(i * 2 + par, par, True)
            for e in (E - 2, E - 1):
                expert_io(e, e % 2, False)
            for t in range(NT):
                sp.wait_ge(o_ready, t + 1)
                sp.dma_start(out[0, t * P:t * P + P, :], x_t[:, t, :]).then_inc(out_done, 16)
            sp.wait_ge(out_done, 16 * NT)

        @block.tensor
        def _(pe):
            mm, tr = nc.tensor.matmul, nc.tensor.transpose
            w3 = wqkv[:].rearrange("p (k c) -> p k c", k=KC)
            pe.sem_inc(pv_done, 2)
            pe.sem_inc(comb_ready, 1)
            pe.sem_inc(at_tr, 2)
            pe.wait_ge(const_in, 16)
            pe.wait_ge(w_in, 48)

            def project_chunk(c, par):
                pe.wait_ge(ln_ready, c + 1)
                pe.wait_ge(xt_lo, c + 1)
                pe.wait_ge(xt_hi, c + 1)
                for k in range(KC):
                    for t in range(TPB):
                        last = tr(bank(k)[:, t * P:t * P + P], xn[par][:, t, k * P:k * P + P], ident)
                    last.then_inc(xt_ready, 1)
                pe.wait_ge(xt_lo, c + 2)
                pe.wait_ge(xt_hi, c + 2)
                for f in range(4):
                    pe.wait_ge(proj_read, 4 * c + f + 1)
                    for k in range(KC):
                        last = mm(bank(2 + f), w3[:, k, f * P:f * P + P], xnT[par][:, k, :], start=k == 0, stop=k == KC - 1)
                    last.then_inc(proj_ready, 1)
                for b in range(2):
                    pe.wait_ge(v_evac, 2 * c + b + 1)
                    for t in (2 * b, 2 * b + 1):
                        for k in range(KC):
                            last = mm(bank(6 + b)[:, (t % 2) * D:(t % 2) * D + D], xnT[par][:, k, t * P:t * P + P],
                                      w3[:, k, 2 * D:3 * D], start=k == 0, stop=k == KC - 1)
                    last.then_inc(v_ready, 1)

            with pe.Fori(0, NQ // 2) as i:
                for par in (0, 1):
                    project_chunk(i * 2 + par, par)

            def score_unit(u, base, qc, kc):
                pe.wait_ge(max_done, base + freed(u))
                qt, ch = u // NCH, u % NCH
                mm(bank(RING + u % RING), q_ring[0:NPR, ds(qc + qt * P, P)], k_ring[0:NPR, ds(kc + ch * QW, QW)],
                   start=True, stop=True).then_inc(s_ready, 1)

            def transpose_maxima(j):
                pe.wait_ge(msplit_ready, j + 1)
                for qt in range(TPB):
                    last = mm(ps[NPR:NAUG, 7 * QW + qt * P:7 * QW + qt * P + P], msplit[:, 4 * qt:4 * qt + 3], identb[:],
                              start=True, stop=True)
                last.then_inc(mt_ready, 1)

            pe.wait_ge(v_evac, 2 * NQ + 2)
            pe.wait_ge(proj_read, 4 * NQ + 4)
            pe.wait_ge(k_in, 96 * K_AHEAD)
            pe.wait_ge(q_in, 96 * Q_AHEAD)
            pe.wait_ge(consts_ready, 3)
            for j in (0, 1):
                for u in range(UNITS):
                    score_unit(u, UNITS * j, j * QW, 0)
                if j == 0:
                    transpose_maxima(0)
            pe.wait_ge(ring_ones, 1)

            def pv_group(it, g):
                pe.wait_ge(exp_done, EXPS * it + 4 * g + 4 + RING)
                if g == 0:
                    pe.wait_ge(o_evac, it + 1)
                    pe.wait_ge(va_in, 16 * (it + 1))
                if g == GROUPS // 2:
                    pe.wait_ge(vb_in, 16 * (it + 1))
                for j in range(4):
                    kt = 4 * g + j
                    last = mm(ps[32 * j:32 * j + 32, 6 * QW:7 * QW], v_sb[:, kt * VW:kt * VW + VW],
                              p_ring[:, kt % 8, :],
                              start=g == 0, stop=g == GROUPS - 1)
                last.then_inc(pv_done, 1)

            def combine(it):
                pe.wait_ge(o_evac, it + 2)
                for qt in range(TPB):
                    last = mm(ps[:, 7 * QW + 32 * qt:7 * QW + 32 * qt + 17], o_sb[:, qt * P:qt * P + P], fold[:, 0:17],
                              start=True, stop=True)
                last.then_inc(comb_ready, 1)

            def attention_step(it, prev=True, scores=True, maxima=True):
                dyn = not isinstance(it, int)
                snap = pe.snap if dyn else (lambda v: v)
                qc, kc = snap((it % QRING) * QW), snap(((it >> 3) % 3) * T)
                qn, kn = snap(((it + 2) % QRING) * QW), snap((((it + 2) >> 3) % 3) * T)
                e0, u0 = snap(it * EXPS), snap((it + 2) * UNITS)
                pe.wait_ge(mrow_ready, it + 1)
                if scores:
                    pe.wait_ge(q_in, 96 * (it + 3))
                    pe.wait_ge(k_in, (((it + 2) >> 3) + 1) * (96 * NQ))

                def keys(kt):
                    pe.wait_ge(exp_done, e0 + freed(kt))
                    mm(bank(kt % RING), k_ring[0:NAUG, ds(kc + kt * P, P)], q_ring[0:NAUG, ds(qc, QW)],
                       start=True, stop=True).then_inc(st_ready, 1)

                def unit(u):
                    if scores:
                        score_unit(u, u0, qn, kn)

                for s in range(GROUPS):
                    if s >= PV_LAG:
                        pv_group(it, s - PV_LAG)
                    elif prev:
                        pv_group(it - 1, s - PV_LAG + GROUPS)
                    for j in range(3):
                        unit(4 * s + j)
                        keys(4 * s + j)
                    if s == 3 and prev:
                        combine(it - 1)
                    if s == 5 and maxima:
                        if prev:
                            pe.wait_ge(comb_done, it)
                        transpose_maxima(it + 1)
                    unit(4 * s + 3)
                    keys(4 * s + 3)

            attention_step(0, prev=False)
            with pe.Fori(1, STEPS - 2) as it:
                attention_step(it)
            attention_step(STEPS - 2, scores=False)
            attention_step(STEPS - 1, scores=False, maxima=False)
            for g in range(GROUPS - PV_LAG, GROUPS):
                pv_group(STEPS - 1, g)
            pe.wait_ge(comb_done, STEPS - 1)
            combine(STEPS - 1)

            wo3 = wout[:].rearrange("p (k c) -> p k c", k=KC)
            wg3 = wgate[:].rearrange("p (k c) -> p k c", k=KC)
            pe.wait_ge(vec_in, 64)

            def turn(t, i, par):
                pe.wait_ge(at_in[par], 16 * (i + 1))
                pe.wait_ge(atT_copied, t + 1)
                for k in range(KC):
                    last = tr(bank(0)[:, k * P:k * P + P], at[par][:, k * P:k * P + P], ident)
                last.then_inc(at_tr, 1)

            def project(t, par):
                pe.wait_ge(atT_copied, t + 2)
                pe.wait_ge(x2_chain, 4 * t + 1)
                for k in range(KC):
                    last = mm(bank(1)[:, 0:D], atT[par][:, k * P:k * P + P], wo3[:, k, :], start=k == 0, stop=k == KC - 1)
                last.then_inc(proj2_ready, 1)

            def turn_normed(t, par):
                pe.wait_ge(xs_ready, t + 1)
                pe.wait_ge(xsT_copied, t + 1)
                for k in range(KC):
                    last = tr(bank(2)[:, k * P:k * P + P], xs[par][:, k * P:k * P + P], ident)
                last.then_inc(xs_tr, 1)

            def gate(t, par):
                pe.wait_ge(xsT_copied, t + 2)
                pe.wait_ge(gate_read, t + 1)
                for k in range(KC):
                    last = mm(bank(3)[:, 0:E], xsT[par][:, k * P:k * P + P], wg3[:, k, :], start=k == 0, stop=k == KC - 1)
                last.then_inc(gate_ready, 1)

            def tile_step(t, i, par):
                turn(t, i, par)
                turn_normed(t - 1, 1 - par)
                project(t, par)
                gate(t - 1, 1 - par)

            turn(0, 0, 0)
            project(0, 0)
            with pe.Fori(0, NT // 2 - 1) as i:
                tile_step(i * 2 + 1, i, 1)
                tile_step(i * 2 + 2, i + 1, 0)
            tile_step(NT - 1, NT // 2 - 1, 1)
            turn_normed(NT - 1, 1)
            gate(NT - 1, 1)

            pe.wait_ge(rank_in, 1)
            mm(bank(4)[:, 0:NT * E], trib[:], maskb, start=True, stop=True)
            mm(bank(5)[:, 0:NT * E], onesb[:], maskb, start=True, stop=True).then_inc(rank_out, 1)

            def turn_slots(e, i, par):
                pe.wait_ge(xin_in[par], 16 * (i + 1))
                pe.wait_ge(xi_lo, e + 1)
                pe.wait_ge(xi_mid, e + 1)
                pe.wait_ge(xi_hi, e + 1)
                for k in range(KC):
                    for s in range(ST):
                        o = (k * ST + s) * P
                        last = tr(ps[:, o:o + P], xin[par][:, s, k * P:k * P + P], ident)
                last.then_inc(xi_tr, 1)

            def layer1(e, i, par):
                pe.wait_ge(we_in[par], 64 * (i + 1))
                pe.wait_ge(xi_lo, e + 2)
                pe.wait_ge(xi_mid, e + 2)
                pe.wait_ge(xi_hi, e + 2)
                for f in range(FT):
                    done = h_act if f % 2 == 0 else h_dve
                    pe.wait_ge(done, FT // 2 * e + f // 2 + 1)
                    for hf in range(2):
                        for k in range(KC):
                            o = k * CAP + hf * CAP // 2
                            last = mm(bank(3 + 2 * (f % 2) + hf)[:, 0:CAP // 2], w1s[par][:, k, f * P:f * P + P],
                                      xinT[par][:, o:o + CAP // 2], start=k == 0, stop=k == KC - 1)
                    last.then_inc(h_ready, 1)

            def layer2(e, par):
                pe.wait_ge(h_act, FT // 2 * e + FT // 2 + 1)
                pe.wait_ge(h_dve, FT // 2 * e + FT // 2 + 1)
                for s in range(ST):
                    pe.wait_ge(y_read, ST * e + s + 1)
                    for f in range(FT):
                        last = mm(y_bank(e, par, s), hT[:, f, s * P:s * P + P], w2s[par][:, f, :],
                                  start=f == 0, stop=f == FT - 1)
                    last.then_inc(y_ready, 1)

            def y_bank(e, par, s):
                return bank(7)[:, 0:D] if (s + par) % 2 == 0 else bank(2)[:, D:2 * D]

            def expert(e, i, par, more):
                layer1(e, i, par)
                if more:
                    turn_slots(e + 1, i + par, 1 - par)
                    pe.wait_ge(xi_hi, e + 3)
                layer2(e, par)

            turn_slots(0, 0, 0)
            with pe.Fori(0, E // 2 - 1) as i:
                for par in (0, 1):
                    expert(i * 2 + par, i, par, True)
            expert(E - 2, E // 2 - 1, 0, True)
            expert(E - 1, E // 2 - 1, 1, False)

        @block.scalar
        def _(act):
            av = nc.scalar.activation
            act.sem_inc(xt_lo, 1)
            act.sem_inc(proj_read, 4)
            act.sem_inc(exp_done, RING)
            act.sem_inc(o_evac, 1)
            act.wait_ge(consts_ready, 3)

            def deviation(n, width):
                act.wait_ge(var_ready, n + 1)
                av(dev[:, 0:width], mv[:].rearrange("p (t s) -> p t s", s=2)[:, 0:width, 1], ACT.Sqrt,
                   bias=eps[:, 0:1]).then_inc(dev_ready, 1)

            def project_chunk(c, i, par):
                act.wait_ge(xt_ready, 2 * c + 1)
                av(xnT[par][:, 0, :], bank(0), ACT.Copy).then_inc(xt_lo, 1)
                act.wait_ge(parts_out[par], 12 * 16 * (i + 1))
                for f in range(4):
                    act.wait_ge(proj_ready, 4 * c + f + 1)
                    if f < 2:
                        act.wait_ge(split_v, 2 * c + f + 1)
                    else:
                        act.wait_ge(split_p, 2 * c + f - 1)
                    scale = SCALE if f < 2 else 1.0
                    av(xf[:, f, :], bank(2 + f), ACT.Identity, bias=bqk[:, f:f + 1], scale=scale)
                    av(parts[par][:, f, 0, :], bank(2 + f), ACT.Identity, bias=bqk[:, f:f + 1],
                       scale=scale).then_inc(proj_read, 1)

            deviation(0, TPB)
            with act.Fori(0, NQ // 2 - 1) as i:
                for par in (0, 1):
                    deviation(i * 2 + par + 1, TPB)
                    project_chunk(i * 2 + par, i, par)
            deviation(NQ - 1, TPB)
            project_chunk(NQ - 2, NQ // 2 - 1, 0)
            project_chunk(NQ - 1, NQ // 2 - 1, 1)

            def copy_maxima(j):
                act.wait_ge(mt_ready, j + 1)
                av(q_ring[NPR:NAUG, ds((j % QRING) * QW, QW)], ps[NPR:NAUG, 7 * QW:8 * QW], ACT.Copy).then_inc(mrow_ready, 1)

            for par in (0, 1):
                act.wait_ge(parts_out[par], 12 * 16 * (NQ // 2 + 1))
            copy_maxima(0)

            def evacuate(it):
                act.wait_ge(pv_done, GROUPS * it + GROUPS + 2)
                act.wait_ge(comb_ready, it + 1)
                av(o_sb[:], bank(6), ACT.Copy).then_inc(o_evac, 1)

            def attention_step(it, prev=True, maxima=True):
                snap = (lambda v: v) if isinstance(it, int) else act.snap
                e0, g0 = snap(it * EXPS), snap(it * GROUPS)
                for n in range(EXPS):
                    act.wait_ge(st_ready, e0 + n + 1)
                    act.wait_ge(pv_done, g0 + n // 4 + 1)
                    av(p_ring[:, n % 8, :], bank(n % RING), ACT.Exp).then_inc(exp_done, 1)
                    if n == 4 * (PV_LAG - 1) + 1 and prev:
                        evacuate(it - 1)
                    if n == 25 and maxima:
                        copy_maxima(it + 1)

            attention_step(0, prev=False)
            with act.Fori(1, STEPS - 1) as it:
                attention_step(it)
            attention_step(STEPS - 1, maxima=False)
            evacuate(STEPS - 1)

            def tile_copies(t, par, first=True, second=True):
                if first:
                    act.wait_ge(at_tr, t + 3)
                    av(atT[par], bank(0)[:, 0:D], ACT.Copy).then_inc(atT_copied, 1)
                if second:
                    act.wait_ge(xs_tr, t)
                    av(xsT[1 - par], bank(2)[:, 0:D], ACT.Copy).then_inc(xsT_copied, 1)
                if first:
                    deviation(NQ + t, 1)

            act.sem_inc(atT_copied, 1)
            act.sem_inc(xsT_copied, 1)
            tile_copies(0, 0, second=False)
            with act.Fori(0, NT // 2 - 1) as i:
                tile_copies(i * 2 + 1, 1)
                tile_copies(i * 2 + 2, 0)
            tile_copies(NT - 1, 1)
            tile_copies(NT, 0, first=False)

            act.wait_ge(exp_in, 1)
            av(rt[2], rt[1], ACT.Exp).then_inc(exp_out, 1)

            act.sem_inc(xi_lo, 1)
            act.sem_inc(h_act, 1)

            def slots_copy(e, par):
                act.wait_ge(xi_tr, e + 1)
                av(xinT[par][:, 0:QW], bank(0), ACT.Copy).then_inc(xi_lo, 1)

            def expert(e, i, par, more):
                act.wait_ge(we_in[par], 64 * (i + 1))
                for f in range(0, FT, 2):
                    act.wait_ge(h_ready, FT * e + f + 1)
                    av(hT[:, f, :].rearrange("p (a c) -> p a c", a=2),
                       bank(3, 2).rearrange("p (a c) -> p a c", a=2)[:, :, 0:CAP // 2], ACT.Relu,
                       bias=b1s[:, FT * par + f:FT * par + f + 1]).then_inc(h_act, 1)
                if more:
                    slots_copy(e + 1, 1 - par)

            slots_copy(0, 0)
            with act.Fori(0, E // 2 - 1) as i:
                for par in (0, 1):
                    expert(i * 2 + par, i, par, True)
            expert(E - 2, E // 2 - 1, 0, True)
            expert(E - 1, E // 2 - 1, 1, False)

        @block.gpsimd
        def _(pool):
            g = nc.gpsimd
            pool.sem_inc(split_p, 2)
            g.memset(zeros[:], 0.0).then_inc(zeros_ready, 1)
            for par in (0, 1):
                g.memset(vst[par][:, :, :, HD:VW], 0.0).then_inc(vst_ready, 1)
                pool.wait_ge(vst_ready, 2 * par + 1)
                g.memset(vst[par][:, :, :, HD:HD + 1], 1.0).then_inc(vst_ready, 1)
            pool.wait_ge(vst_ready, 4)
            g.memset(k_ring[NPR:NAUG, :], 1.0).then_inc(ring_ones, 1)

            pool.wait_ge(ring_ones, 1)

            def split_chunk(c, par):
                link = chain(pool, chain_p, c * 4)
                for f in (2, 3):
                    pool.wait_ge(proj_read, 4 * c + f + 5)
                    link(g.tensor_tensor(res[:, 1, :], xf[:, f, :], parts[par][:, f, 0, :], ALU.subtract))
                    link(g.tensor_copy(parts[par][:, f, 1, :], res[:, 1, :]))
                    g.tensor_tensor(parts[par][:, f, 2, :], res[:, 1, :], parts[par][:, f, 1, :], ALU.subtract).then_inc(split_p, 1)
                    pool.wait_ge(split_p, 2 * c + f + 1)

            with pool.Fori(0, NQ // 2) as i:
                for par in (0, 1):
                    split_chunk(i * 2 + par, par)

            msp = msplit[:].rearrange("p (t n) -> p n t", n=4)

            def split_maxima(j):
                link = chain(pool, split_chain, j * 4)
                pool.wait_ge(mx_ready, j + 1)
                if not isinstance(j, int) or j > 0:
                    pool.wait_ge(mt_ready, j)
                lone_wait(pool)
                link(g.tensor_scalar(mneg[:], mx[:], -1.0, None, ALU.mult))
                link(g.tensor_copy(msp[:, 0, :], mneg[:]))
                link(g.tensor_tensor(mres[:], mneg[:], msp[:, 0, :], ALU.subtract))
                link(g.tensor_copy(msp[:, 1, :], mres[:]))
                g.tensor_tensor(msp[:, 2, :], mres[:], msp[:, 1, :], ALU.subtract).then_inc(msplit_ready, 1)

            split_maxima(0)
            with pool.Fori(1, STEPS) as j:
                split_maxima(j)

            pool.wait_ge(zero_out, 16 * (E * CAP // (2 * P)))
            pool.wait_ge(slots_ready, 2)
            for t in range(NT):
                for j in range(2):
                    g.indirect_dma_start(xin_d, bass.IndirectOffsetOnAxis(slot_w[:, j * NT + t:j * NT + t + 1], 0),
                                         a_t[:, t, :], None, bounds_check=E * CAP - 1, oob_is_err=False).then_inc(scattered, 16)
            pool.wait_ge(y_out[0], 16 * (E // 2 + 1))
            pool.wait_ge(y_out[1], 16 * (E // 2 + 1))
            for t in range(NT):
                if t >= G:
                    pool.wait_ge(o_ready, t - G + 1)
                for j in range(2):
                    g.indirect_dma_start(gat[t % G][j], None, y_d,
                                         bass.IndirectOffsetOnAxis(slot_r[:, j * NT + t:j * NT + t + 1], 0)).then_inc(g_in[t % G], 16)

        @block.vector
        def _(dve):
            v = nc.vector
            dve.sem_inc(xt_hi, 1)
            dve.sem_inc(v_evac, 2)
            dve.sem_inc(split_v, 2)
            dve.sem_inc(max_done, RING)
            dve.wait_ge(const_in, 16)
            dve.wait_ge(w_in, 48)
            v.tensor_scalar(bqk[:, 0:2], bqk[:, 0:2], SCALE, None, ALU.mult).then_inc(consts_ready, 1)
            v.tensor_copy(identb[:], ident)
            v.tensor_copy(trib[:], cst[:, P:2 * P]).then_inc(consts_ready, 1)
            v.memset(eps[:], EPS)
            v.memset(onesb[:], 1.0).then_inc(consts_ready, 1)
            dve.wait_ge(vst_ready, 4)

            st3 = stats[:].rearrange("p (t s) -> p t s", s=6)
            mv3 = mv[:].rearrange("p (t s) -> p t s", s=2)

            def normalise(c, par):
                link = chain(dve, ln_chain, c * 1)
                dve.wait_ge(x_in, 16 * (c + 1))
                lone_wait(dve)
                for t in range(TPB):
                    last = v.bn_stats(st3[:, t, :], x_all[:, ds((c * TPB + t) * D, D)])
                link(last)
                for t in range(TPB):
                    last = v.bn_aggr(mv3[:, t, :], st3[:, t, :])
                last.then_inc(var_ready, 1)
                dve.wait_ge(dev_ready, c + 1)
                v.reciprocal(rstd[:], dev[:]).then_inc(rstd_ready, 1)
                dve.wait_ge(rstd_ready, c + 1)
                for t in range(TPB):
                    last = v.tensor_scalar(xn[par][:, t, :], x_all[:, ds((c * TPB + t) * D, D)], mv3[:, t, 0:1],
                                           rstd[:, t:t + 1], ALU.subtract, ALU.mult)
                last.then_inc(ln_ready, 1)

            def project_chunk(c, i, par):
                dve.wait_ge(xt_ready, 2 * c + 2)
                v.tensor_copy(xnT[par][:, 1, :], bank(1)).then_inc(xt_hi, 1)
                link = Chain(dve, chain_v, c * 4)
                for f in (0, 1):
                    dve.wait_ge(proj_read, 4 * c + f + 5)
                    link(v.tensor_tensor(res[:, 0, :], xf[:, f, :], parts[par][:, f, 0, :], ALU.subtract))
                    link(v.tensor_copy(parts[par][:, f, 1, :], res[:, 0, :]))
                    v.tensor_tensor(parts[par][:, f, 2, :], res[:, 0, :], parts[par][:, f, 1, :], ALU.subtract).then_inc(split_v, 1)
                    dve.wait_ge(split_v, 2 * c + f + 3)
                dve.wait_ge(v_out[par], 16 * (i + 1))
                for b in range(2):
                    dve.wait_ge(v_ready, 2 * c + b + 1)
                    for t in range(2):
                        last = v.tensor_tensor(vst[par][:, :, 2 * b + t, 0:HD],
                                               bank(6 + b)[:, t * D:t * D + D].rearrange("p (h c) -> p h c", h=H),
                                               bv[:].rearrange("p (h c) -> p h c", h=H), ALU.add)
                    last.then_inc(v_evac, 1)

            normalise(0, 0)
            with dve.Fori(0, NQ // 2 - 1) as i:
                normalise(i * 2 + 1, 1)
                project_chunk(i * 2, i, 0)
                normalise(i * 2 + 2, 0)
                project_chunk(i * 2 + 1, i, 1)
            normalise(NQ - 1, 1)
            project_chunk(NQ - 2, NQ // 2 - 1, 0)
            project_chunk(NQ - 1, NQ // 2 - 1, 1)

            sums = ps[:, 7 * QW:7 * QW + 32 * TPB].rearrange("p (t c) -> p t c", t=TPB)

            def maximum(u, base):
                dve.wait_ge(s_ready, base + u + 1)
                v.tensor_reduce(mpart[:, u:u + 1], bank(RING + u % RING), AX.X, ALU.max).then_inc(max_done, 1)

            def reduce_maxima(j):
                dve.wait_ge(max_done, (j + 1) * UNITS + RING)
                if not isinstance(j, int) or j > 0:
                    dve.wait_ge(msplit_ready, j)
                v.tensor_reduce(mx[:], mpart[:].rearrange("p (t c) -> p t c", t=TPB), AX.X, ALU.max).then_inc(mx_ready, 1)
                dve.wait_ge(mx_ready, j + 1)

            def write_rows(it):
                dve.wait_ge(comb_ready, it + 2)
                v.reciprocal(rden[:], sums[:, :, HD]).then_inc(rden_ready, 1)
                dve.wait_ge(rows_out, 16 * (it + 1))
                dve.wait_ge(rden_ready, it + 1)
                v.tensor_tensor(rows[:, ds((it % 2) * TPB * HD, TPB * HD)].rearrange("p (t c) -> p t c", c=HD),
                                sums[:, :, 0:HD], rden[:].unsqueeze(2).to_broadcast([P, TPB, HD]),
                                ALU.mult).then_inc(comb_done, 1)

            for j in (0, 1):
                for u in range(UNITS):
                    maximum(u, UNITS * j)
                if j == 0:
                    reduce_maxima(0)

            def attention_step(it, prev=True, scores=True, maxima=True):
                snap = (lambda x_: x_) if isinstance(it, int) else dve.snap
                u0 = snap((it + 2) * UNITS)
                if maxima:
                    reduce_maxima(it + 1)
                for u in range(UNITS):
                    if scores:
                        maximum(u, u0)
                    if u == 17 and prev:
                        write_rows(it - 1)

            attention_step(0, prev=False)
            with dve.Fori(1, STEPS - 2) as it:
                attention_step(it)
            attention_step(STEPS - 2, scores=False)
            attention_step(STEPS - 1, scores=False, maxima=False)
            write_rows(STEPS - 1)

            dve.wait_ge(vec_in, 64)
            dve.sem_inc(x2_chain, 4)
            logits = rt[0]
            mvt, stt_ = mv[:, 0:2], stats[:, 0:6]

            def residual(t, par):
                link = chain(dve, x2_chain, t * 4 + 4)
                dve.wait_ge(proj2_ready, t + 1)
                link(v.tensor_tensor(xs[par], bank(1)[:, 0:D], bout[:], ALU.add))
                link(v.tensor_tensor(x_all[:, ds(t * D, D)], xs[par], x_all[:, ds(t * D, D)], ALU.add))
                link(v.bn_stats(stt_, x_all[:, ds(t * D, D)]))
                v.bn_aggr(mvt, stt_).then_inc(var_ready, 1)
                dve.wait_ge(dev_ready, NQ + t + 1)
                v.reciprocal(rstd[:, 0:1], dev[:, 0:1]).then_inc(rstd_ready, 1)
                dve.wait_ge(rstd_ready, NQ + t + 1)
                link(v.tensor_scalar(a_all[:, ds(t * D, D)], x_all[:, ds(t * D, D)], mv[:, 0:1], rstd[:, 0:1],
                                     ALU.subtract, ALU.mult))
                v.tensor_scalar(xs[par], x_all[:, ds(t * D, D)], mv[:, 0:1], rstd[:, 0:1],
                                ALU.subtract, ALU.mult).then_inc(xs_ready, 1)

            def read_gate(t):
                dve.wait_ge(gate_ready, t + 1)
                v.tensor_tensor(arena[:, ds(t * E, E)], bank(3)[:, 0:E], bgate[:], ALU.add).then_inc(gate_read, 1)

            dve.sem_inc(gate_read, 1)
            dve.wait_ge(q_in, 96 * (STEPS + Q_AHEAD))
            dve.wait_ge(k_in, 96 * (STEPS + K_AHEAD))
            residual(0, 0)
            with dve.Fori(0, NT // 2 - 1) as i:
                for par in (1, 0):
                    t = i * 2 + (1 if par else 2)
                    residual(t, par)
                    read_gate(t - 1)
            residual(NT - 1, 1)
            read_gate(NT - 2)
            read_gate(NT - 1)
            dve.wait_ge(gate_read, NT + 1)

            link = Chain(dve, route_chain)

            def wide(a):
                return a.unsqueeze(2).to_broadcast([P, NT, E])

            ex = iota_e.unsqueeze(1).to_broadcast([P, NT, E])
            rmax, rsum, rrec = r1[0], r1[1], r1[2]
            link(v.tensor_reduce(rmax, logits, AX.X, ALU.max))
            v.tensor_tensor(rt[1], logits, wide(rmax), ALU.subtract).then_inc(exp_in, 1)
            dve.wait_ge(exp_out, 1)
            link(v.tensor_reduce(rsum, rt[2], AX.X, ALU.add))
            link(v.reciprocal(rrec, rsum))
            link(v.tensor_tensor(rt[3], rt[2], wide(rrec), ALU.mult))
            prob = rt[3]
            sel = []
            for n in range(2):
                top, idx = r1[3 + n], r1[5 + n]
                link(v.tensor_reduce(top, prob, AX.X, ALU.max))
                link(v.tensor_tensor(rt[4], prob, wide(top), ALU.is_lt))
                link(v.scalar_tensor_tensor(rt[5], rt[4], float(E), ex, ALU.mult, ALU.add))
                link(v.tensor_reduce(idx, rt[5], AX.X, ALU.min))
                pick = rt[6 + n]
                link(v.tensor_tensor(pick, ex, wide(idx), ALU.is_equal))
                sel.append(pick)
                if n == 0:
                    link(v.scalar_tensor_tensor(rt[8], pick, -2.0, prob, ALU.mult, ALU.add))
                    prob = rt[8]
            v.tensor_tensor(maskb.rearrange("p (t e) -> p t e", e=E), sel[0], sel[1], ALU.add).then_inc(rank_in, 1)
            dve.wait_ge(rank_out, 1)
            tot = [rt[9], rt[10]]
            link(v.tensor_copy(tot[0], bank(5)[:, 0:NT * E].rearrange("p (t e) -> p t e", e=E)))
            cur, step = 0, 1
            while step < NT:
                a, b = tot[cur], tot[1 - cur]
                link(v.tensor_copy(b[:, 0:step, :], a[:, 0:step, :]))
                link(v.tensor_tensor(b[:, step:NT, :], a[:, step:NT, :], a[:, 0:NT - step, :], ALU.add))
                cur, step = 1 - cur, 2 * step
            rank, slot = rt[11], rt[12]
            link(v.tensor_copy(rank, bank(4)[:, 0:NT * E].rearrange("p (t e) -> p t e", e=E)))
            link(v.tensor_tensor(rank[:, 1:NT, :], rank[:, 1:NT, :], tot[cur][:, 0:NT - 1, :], ALU.add))
            over = rt[13]
            link(v.tensor_scalar(over, rank, float(CAP), None, ALU.is_gt))
            link(v.tensor_tensor(slot, rank, slot_base.unsqueeze(1).to_broadcast([P, NT, E]), ALU.add))
            den = r1[7]
            link(v.tensor_tensor(den, r1[3], r1[4], ALU.add))
            link(v.reciprocal(den, den))
            for n in range(2):
                s_n, o_n, f_n = r1[8 + n], r1[10 + n], r1[12 + n]
                link(v.tensor_tensor(rt[14], sel[n], slot, ALU.mult))
                link(v.tensor_reduce(s_n, rt[14], AX.X, ALU.add))
                link(v.tensor_tensor(rt[15], sel[n], over, ALU.mult))
                link(v.tensor_reduce(o_n, rt[15], AX.X, ALU.add))
                link(v.scalar_tensor_tensor(f_n, o_n, BIG, s_n, ALU.mult, ALU.add))
                link(v.tensor_copy(slot_w[:, n * NT:n * NT + NT], f_n))
                link(v.tensor_scalar(s_n, s_n, float(E * CAP - 1), None, ALU.min))
                link(v.tensor_copy(slot_r[:, n * NT:n * NT + NT], s_n))
                link(v.tensor_scalar(o_n, o_n, -1.0, 1.0, ALU.mult, ALU.add))
                link(v.tensor_tensor(f_n, r1[3 + n], den, ALU.mult))
                v.tensor_tensor(wgt[:, n * NT:n * NT + NT], f_n, o_n, ALU.mult).then_inc(slots_ready, 1)

            dve.sem_inc(xi_mid, 1)
            dve.sem_inc(xi_hi, 1)
            dve.sem_inc(h_dve, 1)
            dve.sem_inc(y_read, 2)

            def slots_copy(e, par):
                dve.wait_ge(xi_tr, e + 1)
                v.tensor_copy(xinT[par][:, QW:2 * QW], bank(1)).then_inc(xi_mid, 1)
                v.tensor_copy(xinT[par][:, 2 * QW:2 * CAP], bank(2)[:, 0:2 * CAP - 2 * QW]).then_inc(xi_hi, 1)

            def expert(e, i, par, more):
                dve.wait_ge(we_in[par], 64 * (i + 1))
                for f in range(1, FT, 2):
                    dve.wait_ge(h_ready, FT * e + f + 1)
                    v.tensor_scalar(hT[:, f, :].rearrange("p (a c) -> p a c", a=2),
                                    bank(5, 2).rearrange("p (a c) -> p a c", a=2)[:, :, 0:CAP // 2],
                                    b1s[:, FT * par + f:FT * par + f + 1], 0.0, ALU.add, ALU.max).then_inc(h_dve, 1)
                if more:
                    slots_copy(e + 1, 1 - par)
                dve.wait_ge(y_out[par], 16 * (i + 1))
                for s in range(ST):
                    src = bank(7)[:, 0:D] if (s + par) % 2 == 0 else bank(2)[:, D:2 * D]
                    dve.wait_ge(y_ready, ST * e + s + 1)
                    v.tensor_tensor(ys[par][:, s, :], src, b2s[:, D * par:D * par + D], ALU.add).then_inc(y_read, 1)

            slots_copy(0, 0)
            with dve.Fori(0, E // 2 - 1) as i:
                for par in (0, 1):
                    expert(i * 2 + par, i, par, True)
            expert(E - 2, E // 2 - 1, 0, True)
            expert(E - 1, E // 2 - 1, 1, False)

            for t in range(NT):
                dve.wait_ge(g_in[t % G], 32 * (t // G + 1))
                v.scalar_tensor_tensor(x_t[:, t, :], gat[t % G][0], wgt[:, t:t + 1], x_t[:, t, :],
                                       ALU.mult, ALU.add).then_inc(o_chain, 1)
                dve.wait_ge(o_chain, t + 1)
                v.scalar_tensor_tensor(x_t[:, t, :], gat[t % G][1], wgt[:, NT + t:NT + t + 1], x_t[:, t, :],
                                       ALU.mult, ALU.add).then_inc(o_ready, 1)


INPUTS = ["L0_attn_x", "L0_attn_W_qkv", "L0_attn_b_qkv", "L0_attn_W_out", "L0_attn_b_out", "L0_ffn_gate_w",
          "L0_ffn_gate_b", "L0_ffn_w1", "L0_ffn_b1", "L0_ffn_w2", "L0_ffn_b2"]


def constants():
    c = np.zeros((P, CW), np.float32)
    c[:, 0:P] = np.eye(P)
    c[:, P:2 * P] = np.triu(np.ones((P, P)))
    c[:, 2 * P:2 * P + 32] = np.tile(np.eye(32), (4, 1))
    c[:, 2 * P + 32:2 * P + 32 + E] = np.arange(E)
    c[:, 2 * P + 32 + E:] = np.arange(E) * CAP - 1
    return c


def kernel(**inputs):
    import concourse.bacc as bacc
    from concourse.bass_utils import run_bass_kernel_spmd

    nc = bacc.Bacc("TRN2", target_bir_lowering=False, num_devices=1)
    arrays = {name: np.ascontiguousarray(inputs[name]) for name in INPUTS}
    arrays["consts"] = constants()
    aps = [nc.dram_tensor(n, a.shape, mybir.dt.from_np(a.dtype), kind="ExternalInput").ap() for n, a in arrays.items()]
    out = nc.dram_tensor("out", (1, T, D), F32, kind="ExternalOutput").ap()
    build(nc, *aps, out)
    r = run_bass_kernel_spmd(nc, [arrays], core_ids=[0])
    return r.results[0]["out"]
```

```python
from contextlib import ExitStack

import numpy as np

import concourse.bass as bass
from concourse import mybir

F32 = mybir.dt.float32
BF16 = mybir.dt.bfloat16
U32 = mybir.dt.uint32
ALU = mybir.AluOpType
ACT = mybir.ActivationFunctionType
AX = mybir.AxisListType
ds = bass.ds

P = 128
T, D, H, HD = 4096, 256, 16, 16
NT = T // P
QW = 512
NQ = T // QW
TPB = QW // P
STEPS = H * NQ
NCH = T // QW
E, FF = 8, 1024
CAP = int(1.25 * T / E)
ST = CAP // P
KC = D // P
FT = FF // P
EPS = 1e-5
SCALE = 1.0 / float(np.sqrt(HD))
Q_PARTS = (0, 1, 2, 0, 1, 0)
K_PARTS = (0, 0, 0, 1, 1, 2)
NPR = 16 * len(Q_PARTS)
NAUG = NPR + 3
QRING, KRING = 16, 24
Q_AHEAD, K_AHEAD = 4, 12
VW = 32
EXPS = T // P
UNITS = TPB * NCH
RING = 3
GROUPS = T // (4 * P)
PV_LAG = 2
BIG = 1.0e6
CW = P + P + E + E


def freed(n):
    assert EXPS % RING == 2 and UNITS % RING == 2
    return n + 1 if n >= 2 else n + 2


class Chain:

    def __init__(self, eng, sem, base=0):
        self.eng, self.sem, self.n = eng, sem, base

    def __call__(self, ins):
        ins.then_inc(self.sem, 1)
        self.n = self.n + 1
        self.eng.wait_ge(self.sem, self.n)


def build(nc, x, w_qkv, b_qkv, w_out, b_out, gate_w, gate_b, w1, b1, w2, b2, consts, out):
    qk_d = nc.dram_tensor("qk_parts", (2, 3, D, T), BF16, kind="Internal").ap()
    v_d = nc.dram_tensor("v_heads", (H, P, NT * VW), F32, kind="Internal").ap()
    att_d = nc.dram_tensor("attention_rows", (STEPS * QW, HD), F32, kind="Internal").ap()
    xin_d = nc.dram_tensor("expert_in", (E * CAP, D), F32, kind="Internal").ap()
    y_d = nc.dram_tensor("expert_out", (E * CAP, D), F32, kind="Internal").ap()

    with ExitStack() as ctx:
        def sb(name, cols, dt=F32):
            return ctx.enter_context(nc.sbuf_tensor(name, [P, cols], dt))

        def sem(name):
            return ctx.enter_context(nc.semaphore(name))

        cst = sb("cst", CW)
        ident = cst[:, 0:P]
        iota_e = cst[:, 2 * P:2 * P + E]
        slot_base = cst[:, 2 * P + E:CW]
        identb = sb("identb", P, BF16)
        trib = sb("trib", P, BF16)
        onesb = sb("onesb", P, BF16)
        x_all = sb("x_all", NT * D)
        a_all = sb("a_all", NT * D)
        arena = sb("arena", (KRING + QRING) * QW // 2 + 4096)
        extra = sb("extra", 2048)
        wbuf = sb("wbuf", 8192)
        v_sb = sb("v_sb", NT * VW)
        o_sb = sb("o_sb", QW)
        wqkv = sb("wqkv", KC * 3 * D)
        wout = sb("wout", KC * D)
        wgate = sb("wgate", KC * E)
        bqk = sb("bqk", 4)
        bv = sb("bv", D)
        bout = sb("bout", D)
        bgate = sb("bgate", E)
        b1s = sb("b1s", 2 * FT)
        b2s = sb("b2s", 2 * D)
        stats = sb("stats", TPB * 6)
        mv = sb("mv", TPB * 2)
        rstd = sb("rstd", TPB)
        dev = sb("dev", TPB)
        eps = sb("eps", 1)
        mpart = sb("mpart", 2 * UNITS)
        mx = sb("mx", TPB)
        mneg = sb("mneg", TPB)
        mres = sb("mres", TPB)
        msplit = sb("msplit", TPB * 4, BF16)
        osum = sb("osum", TPB * (HD + 1))
        rden = sb("rden", TPB)
        zeros = sb("zeros", 2 * D)
        rows = sb("rows", 2 * TPB * HD)

        x_t = x_all[:].rearrange("p (t c) -> p t c", t=NT)
        a_t = a_all[:].rearrange("p (t c) -> p t c", t=NT)
        kcols, qcols = KRING * QW // 2, QRING * QW // 2
        k_ring = arena[:, 0:kcols].bitcast(BF16)
        q_ring = arena[:, kcols:kcols + qcols].bitcast(BF16)
        p_ring = arena[:, kcols + qcols:kcols + qcols + 4096].rearrange("p (s c) -> p s c", s=8)
        parts = [arena[:, o:o + 3072].bitcast(BF16).rearrange("p (f n c) -> p f n c", f=4, n=3)
                 for o in (kcols, kcols + 3072)]
        res = arena[:, kcols + 6144:kcols + 7168].rearrange("p (s c) -> p s c", s=2)
        vst = [wbuf[:, o:o + 2048].rearrange("p (h t c) -> p h t c", h=H, t=TPB) for o in (0, 2048)]
        xf = wbuf[:, 4096:6144].rearrange("p (f c) -> p f c", f=4)
        xn = [wbuf[:, 6144:7168].rearrange("p (t c) -> p t c", t=TPB),
              wbuf[:, 7168:8192].rearrange("p (t c) -> p t c", t=TPB)]
        xnT = [extra[:, 1024 * i:1024 * i + 1024].rearrange("p (k c) -> p k c", k=KC) for i in (0, 1)]
        at = [arena[:, 6400 + 1024 * i:7424 + 1024 * i].rearrange("p (t c) -> p t c", t=TPB) for i in (0, 1)]
        atT = [arena[:, 8448 + 1024 * i:9472 + 1024 * i] for i in (0, 1)]
        xs = [arena[:, 10496 + 1024 * i:11520 + 1024 * i].rearrange("p (t c) -> p t c", t=TPB) for i in (0, 1)]
        xsT = [extra[:, 1024 * i:1024 * i + 1024] for i in (0, 1)]
        w1s = [wbuf[:, 4096 * i:4096 * i + 2048].rearrange("p (k f) -> p k f", k=KC) for i in (0, 1)]
        w2s = [wbuf[:, 4096 * i + 2048:4096 * i + 4096].rearrange("p (k c) -> p k c", k=FT) for i in (0, 1)]
        xin = [arena[:, 1280 * i:1280 * i + 1280].rearrange("p (s c) -> p s c", s=ST) for i in (0, 1)]
        xinT = [arena[:, 2560 + 1280 * i:3840 + 1280 * i] for i in (0, 1)]
        ys = [arena[:, 5120 + 1280 * i:6400 + 1280 * i].rearrange("p (s c) -> p s c", s=ST) for i in (0, 1)]
        hT = arena[:, 7680:7680 + FT * CAP].rearrange("p (f c) -> p f c", f=FT)
        rt = [arena[:, 256 * i:256 * i + 256].rearrange("p (t e) -> p t e", e=E) for i in range(20)]
        r1 = [arena[:, 5120 + 32 * i:5152 + 32 * i] for i in range(20)]
        maskb = arena[:, 6144:6272].bitcast(BF16)
        wgt = sb("wgt", 2 * NT)
        slot_w = sb("slot_w", 2 * NT, U32)
        slot_r = sb("slot_r", 2 * NT, U32)
        G = 4
        gat = [[arena[:, 1024 + 256 * (2 * i + j):1280 + 256 * (2 * i + j)] for j in (0, 1)] for i in range(G)]

        ps = ctx.enter_context(nc.psum_tensor("ps", [P, 8 * QW], F32))

        def bank(b, n=1):
            return ps[:, b * QW:(b + n) * QW]

        const_in, x_in, w_in, vec_in = sem("const_in"), sem("x_in"), sem("w_in"), sem("vec_in")
        consts_ready, zeros_ready, vst_ready = sem("consts_ready"), sem("zeros_ready"), sem("vst_ready")
        zero_out = sem("zero_out")
        ln_chain, ln_ready = sem("ln_chain"), sem("ln_ready")
        xt_ready, xt_lo, xt_hi = sem("xt_ready"), sem("xt_lo"), sem("xt_hi")
        proj_ready, proj_read, v_ready, v_evac = sem("proj_ready"), sem("proj_read"), sem("v_ready"), sem("v_evac")
        split_v, split_p, chain_v, chain_p = sem("split_v"), sem("split_p"), sem("chain_v"), sem("chain_p")
        parts_out = [sem("parts_out0"), sem("parts_out1")]
        v_out = [sem("v_out0"), sem("v_out1")]
        ring_ones = sem("ring_ones")
        q_in, k_in, va_in, vb_in = sem("q_in"), sem("k_in"), sem("va_in"), sem("vb_in")
        st_ready, exp_done, pv_done = sem("st_ready"), sem("exp_done"), sem("pv_done")
        s_ready, max_done, mx_ready = sem("s_ready"), sem("max_done"), sem("mx_ready")
        split_chain, msplit_ready, mt_ready, mrow_ready = sem("split_chain"), sem("msplit_ready"), sem("mt_ready"), sem("mrow_ready")
        o_evac, o_turned, osum_ready = sem("o_evac"), sem("o_turned"), sem("osum_ready")
        rden_ready, rows_ready = sem("rden_ready"), sem("rows_ready")
        at_in, at_tr, atT_copied, proj2_ready = [sem("at_in0"), sem("at_in1")], sem("at_tr"), sem("atT_copied"), sem("proj2_ready")
        rows_out = sem("rows_out")
        x2_chain, xs_ready, xs_tr, xsT_copied = sem("x2_chain"), sem("xs_ready"), sem("xs_tr"), sem("xsT_copied")
        x_biased, xs_kept = sem("x_biased"), sem("xs_kept")
        gate_ready, gate_read = sem("gate_ready"), sem("gate_read")
        route_chain, exp_in, exp_out, rank_in, rank_out = sem("route_chain"), sem("gexp_in"), sem("gexp_out"), sem("rank_in"), sem("rank_out")
        slots_ready, scattered = sem("slots_ready"), sem("scattered")
        we_in = [sem("we_in0"), sem("we_in1")]
        xin_in = [sem("xin_in0"), sem("xin_in1")]
        xi_tr, xi_lo, xi_mid, xi_hi = sem("xi_tr"), sem("xi_lo"), sem("xi_mid"), sem("xi_hi")
        h_ready, h_act, h_dve = sem("h_ready"), sem("h_act"), sem("h_dve")
        y_ready, y_read, y_out = sem("y_ready"), sem("y_read"), [sem("y_out0"), sem("y_out1")]
        g_in = [sem(f"g_in{i}") for i in range(G)]
        o_chain, o_ready, out_done = sem("o_chain"), sem("o_ready"), sem("out_done")

        def lone_wait(eng):
            eng.sem_inc(waits_met, 1)

        def chain(eng, done, base):
            link = Chain(eng, done, base)

            def step(ins):
                link(ins)
                lone_wait(eng)
            return step

        var_ready, waits_met = sem("var_ready"), sem("waits_met")
        rstd_ready, dev_ready = sem("rstd_ready"), sem("dev_ready")
        block = ctx.enter_context(nc.Block())

        @block.sync
        def _(sp):
            for par in (0, 1):
                sp.sem_inc(parts_out[par], 12 * 16)
                sp.sem_inc(v_out[par], 16)
                sp.sem_inc(y_out[par], 16)
                sp.sem_inc(rows_out, 16)
            sp.dma_start(cst[:], consts).then_inc(const_in, 16)
            x_tiles = x[0].rearrange("(b t p) c -> b p t c", t=TPB, p=P)
            for b in range(NQ):
                sp.dma_start(x_t[:, TPB * b:TPB * b + TPB, :], x_tiles[b]).then_inc(x_in, 16)
                if b == 0:
                    sp.dma_start(wqkv[:].rearrange("p (k c) -> p k c", k=KC),
                                 w_qkv.rearrange("(k p) c -> p k c", p=P)).then_inc(w_in, 16)
                    sp.dma_start(bqk[:], b_qkv[0:2 * D].rearrange("(f p) -> p f", p=P), allow_slow_non_contiguous=True).then_inc(w_in, 16)
                    sp.dma_start(bv[:], b_qkv[2 * D:3 * D].partition_broadcast(P)).then_inc(w_in, 16)
                sp.wait_ge(x_in, 16 * (b + 1))
            sp.dma_start(wout[:].rearrange("p (k c) -> p k c", k=KC),
                         w_out.rearrange("(k p) c -> p k c", p=P)).then_inc(vec_in, 16)
            sp.dma_start(wgate[:].rearrange("p (k c) -> p k c", k=KC),
                         gate_w.rearrange("(k p) c -> p k c", p=P)).then_inc(vec_in, 16)
            sp.dma_start(bout[:], b_out.partition_broadcast(P)).then_inc(vec_in, 16)
            sp.dma_start(bgate[:], gate_b.partition_broadcast(P)).then_inc(vec_in, 16)
            sp.wait_ge(zeros_ready, 1)
            for i in range(E * CAP // (2 * P)):
                sp.dma_start(xin_d[2 * P * i:2 * P * i + 2 * P, :].rearrange("(p r) c -> p (r c)", r=2),
                             zeros[:]).then_inc(zero_out, 16)

            def store_chunk(c, par):
                for f in range(4):
                    if f < 2:
                        sp.wait_ge(split_v, 2 * c + f + 3)
                    else:
                        sp.wait_ge(split_p, 2 * c + f + 1)
                    for n in range(3):
                        sp.dma_start(qk_d[f // 2, n, (f % 2) * P:(f % 2) * P + P, ds(c * QW, QW)],
                                     parts[par][:, f, n, :]).then_inc(parts_out[par], 16)
                sp.wait_ge(v_evac, 2 * c + 4)
                sp.dma_start(v_d[:, :, ds(c * TPB * VW, TPB * VW)].rearrange("h p c -> p h c"),
                             vst[par].rearrange("p h t c -> p h (t c)")).then_inc(v_out[par], 16)

            def load_q(j):
                for b, part in enumerate(Q_PARTS):
                    sp.dma_start(q_ring[16 * b:16 * b + 16, ds((j % QRING) * QW, QW)],
                                 qk_d[0, part, ds(((j >> 3) % H) * HD, HD), ds((j % NQ) * QW, QW)]).then_inc(q_in, 16)

            def load_k(j):
                for b, part in enumerate(K_PARTS):
                    sp.dma_start(k_ring[16 * b:16 * b + 16, ds((j % KRING) * QW, QW)],
                                 qk_d[1, part, ds(((j >> 3) % H) * HD, HD), ds((j % NQ) * QW, QW)]).then_inc(k_in, 16)

            half = NT * VW // 2

            def load_v(head, second, done):
                o = half if second else 0
                sp.dma_start(v_sb[:, o:o + half], v_d[ds(head, 1), :, o:o + half].rearrange("h p c -> (h p) c")).then_inc(done, 16)

            def load_first_keys(c0, c1):
                for b, part in enumerate(K_PARTS):
                    sp.dma_start(k_ring[16 * b:16 * b + 16, c0 * QW:c1 * QW],
                                 qk_d[1, part, 0:HD, c0 * QW:c1 * QW]).then_inc(k_in, 16)

            with sp.Fori(0, NQ // 2 - 1) as i:
                for par in (0, 1):
                    store_chunk(i * 2 + par, par)
            for par in (0, 1):
                sp.wait_ge(parts_out[par], 12 * 16 * (NQ // 2))
            sp.sem_inc(k_in, 96 * (NQ - 2))
            load_first_keys(0, NQ - 2)
            for par in (0, 1):
                store_chunk(NQ - 2 + par, par)
            for par in (0, 1):
                sp.wait_ge(parts_out[par], 12 * 16 * (NQ // 2 + 1))
            load_first_keys(NQ - 2, NQ)
            sp.sem_inc(q_in, 96 * (Q_AHEAD - 1))
            for b, part in enumerate(Q_PARTS):
                sp.dma_start(q_ring[16 * b:16 * b + 16, 0:Q_AHEAD * QW],
                             qk_d[0, part, 0:HD, 0:Q_AHEAD * QW]).then_inc(q_in, 16)
            for par in (0, 1):
                sp.wait_ge(v_out[par], 16 * (NQ // 2 + 1))
            load_v(0, False, va_in)
            sp.wait_ge(k_in, 96 * NQ)
            sp.wait_ge(q_in, 96 * Q_AHEAD)
            for j in range(NQ, K_AHEAD):
                load_k(j)

            def store_rows(it):
                sp.wait_ge(rows_ready, it + 1)
                lone_wait(sp)
                sp.wait_ge(rows_out, 16 * (it + 2))
                sp.dma_start(att_d[ds(it * QW, QW), :].rearrange("(t p) c -> p t c", p=P),
                             rows[:, ds((it % 2) * TPB * HD, TPB * HD)].rearrange("p (t c) -> p t c", c=HD)
                             ).then_inc(rows_out, 16)

            def attention_loads(it):
                sp.wait_ge(q_in, 96 * (it + Q_AHEAD))
                lone_wait(sp)
                sp.wait_ge(k_in, 96 * (it + K_AHEAD))
                lone_wait(sp)
                if not isinstance(it, int) or it > 0:
                    sp.wait_ge(st_ready, EXPS * it)
                    lone_wait(sp)
                load_q(it + Q_AHEAD)
                load_k(it + K_AHEAD)
                sp.wait_ge(pv_done, GROUPS * it + 2)
                load_v((it >> 3) % H, True, vb_in)
                sp.wait_ge(pv_done, GROUPS * it + GROUPS // 2 + 2)
                load_v(((it + 1) >> 3) % H, False, va_in)
                if not isinstance(it, int) or it > 0:
                    store_rows(it - 1)

            def load_expert(e, par):
                sp.dma_start(w1s[par], w1[ds(e, 1)].rearrange("e (k p) f -> p (e k) f", p=P)).then_inc(we_in[par], 16)
                sp.dma_start(w2s[par], w2[ds(e, 1)].rearrange("e (k p) c -> p (e k) c", p=P)).then_inc(we_in[par], 16)
                sp.dma_start(b1s[:, FT * par:FT * par + FT],
                             b1[ds(e, 1)].rearrange("e (f p) -> p (e f)", p=P), allow_slow_non_contiguous=True).then_inc(we_in[par], 16)
                sp.dma_start(b2s[:, D * par:D * par + D],
                             b2[ds(e, 1)].rearrange("e c -> (e c)").partition_broadcast(P)).then_inc(we_in[par], 16)

            load_expert(0, 0)
            load_expert(1, 1)
            attention_loads(0)
            with sp.Fori(1, STEPS) as it:
                attention_loads(it)
            store_rows(STEPS - 1)
            sp.wait_ge(q_in, 96 * (STEPS + Q_AHEAD))
            sp.wait_ge(k_in, 96 * (STEPS + K_AHEAD))
            sp.wait_ge(va_in, 16 * (STEPS + 1))
            sp.wait_ge(rows_out, 16 * (STEPS + 2))

            def load_rows(c, par):
                sp.wait_ge(at_tr, c + 1)
                sp.dma_start(at[par], att_d[ds(c * QW * D // HD, QW * D // HD), :].rearrange("(t p k) c -> p t (k c)", p=P, t=TPB)
                             ).then_inc(at_in[par], 16)

            with sp.Fori(0, NQ // 2) as i:
                for par in (0, 1):
                    load_rows(i * 2 + par, par)

            def load_slots(e, par):
                sp.dma_start(xin[par], xin_d[ds(e * CAP, CAP), :].rearrange("(s p) c -> p s c", p=P)).then_inc(xin_in[par], 16)

            sp.wait_ge(scattered, 16 * 2 * NT)
            load_slots(0, 0)
            load_slots(1, 1)

            def expert_io(e, par, more):
                sp.wait_ge(y_read, ST * (e + 1) + 2)
                sp.dma_start(y_d[ds(e * CAP, CAP), :].rearrange("(s p) c -> p s c", p=P), ys[par]).then_inc(y_out[par], 16)
                if more:
                    load_expert(e + 2, par)
                    load_slots(e + 2, par)

            with sp.Fori(0, E // 2 - 1) as i:
                for par in (0, 1):
                    expert_io(i * 2 + par, par, True)
            for e in (E - 2, E - 1):
                expert_io(e, e % 2, False)
            for t in range(NT):
                sp.wait_ge(o_ready, t + 1)
                sp.dma_start(out[0, t * P:t * P + P, :], x_t[:, t, :]).then_inc(out_done, 16)
            sp.wait_ge(out_done, 16 * NT)

        @block.tensor
        def _(pe):
            mm, tr = nc.tensor.matmul, nc.tensor.transpose
            w3 = wqkv[:].rearrange("p (k c) -> p k c", k=KC)
            pe.sem_inc(pv_done, 2)
            pe.sem_inc(o_turned, 1)
            pe.sem_inc(at_tr, 2)
            pe.wait_ge(const_in, 16)
            pe.wait_ge(w_in, 48)

            def turn_chunk(c, par):
                pe.wait_ge(ln_ready, c + 1)
                pe.wait_ge(xt_lo, c + 1)
                pe.wait_ge(xt_hi, c + 1)
                for k in range(KC):
                    for t in range(TPB):
                        last = tr(bank(k)[:, t * P:t * P + P], xn[par][:, t, k * P:k * P + P], ident)
                    last.then_inc(xt_ready, 1)

            def project_features(c, par):
                pe.wait_ge(xt_lo, c + 2)
                pe.wait_ge(xt_hi, c + 2)
                for f in range(4):
                    pe.wait_ge(proj_read, 4 * c + f + 1)
                    for k in range(KC):
                        last = mm(bank(2 + f), w3[:, k, f * P:f * P + P], xnT[par][:, k, :], start=k == 0, stop=k == KC - 1)
                    last.then_inc(proj_ready, 1)

            def project_values(c, par):
                for b in range(2):
                    pe.wait_ge(v_evac, 2 * c + b + 1)
                    for t in (2 * b, 2 * b + 1):
                        for k in range(KC):
                            last = mm(bank(6 + b)[:, (t % 2) * D:(t % 2) * D + D], xnT[par][:, k, t * P:t * P + P],
                                      w3[:, k, 2 * D:3 * D], start=k == 0, stop=k == KC - 1)
                    last.then_inc(v_ready, 1)

            def project_chunk(c, par, more=True):
                project_features(c, par)
                if more:
                    turn_chunk(c + 1, 1 - par)
                project_values(c, par)

            turn_chunk(0, 0)
            with pe.Fori(0, NQ // 2 - 1) as i:
                for par in (0, 1):
                    project_chunk(i * 2 + par, par)
            project_chunk(NQ - 2, 0)
            project_chunk(NQ - 1, 1, more=False)

            def score_unit(u, base, qc, kc):
                pe.wait_ge(max_done, base + freed(u))
                qt, ch = u // NCH, u % NCH
                mm(bank(RING + u % RING), q_ring[0:NPR, ds(qc + qt * P, P)], k_ring[0:NPR, ds(kc + ch * QW, QW)],
                   start=True, stop=True).then_inc(s_ready, 1)

            def transpose_maxima(j):
                pe.wait_ge(msplit_ready, j + 1)
                for qt in range(TPB):
                    last = mm(ps[NPR:NAUG, 7 * QW + qt * P:7 * QW + qt * P + P], msplit[:, 4 * qt:4 * qt + 3], identb[:],
                              start=True, stop=True)
                last.then_inc(mt_ready, 1)

            pe.wait_ge(v_evac, 2 * NQ + 2)
            pe.wait_ge(proj_read, 4 * NQ + 4)
            pe.wait_ge(k_in, 96 * NQ)
            pe.wait_ge(q_in, 96 * Q_AHEAD)
            pe.wait_ge(consts_ready, 3)
            for j in (0, 1):
                for u in range(UNITS):
                    score_unit(u, UNITS * j, j * QW, 0)
                    if j == 1 and u == 12:
                        transpose_maxima(0)
            pe.wait_ge(ring_ones, 1)

            def pv_group(it, e0, g):
                pe.wait_ge(exp_done, e0 + (4 * g + 4 + RING))
                if g == 0:
                    pe.wait_ge(o_evac, it + 1)
                    pe.wait_ge(va_in, 16 * (it + 1))
                if g == GROUPS // 2:
                    pe.wait_ge(vb_in, 16 * (it + 1))
                for j in range(4):
                    kt = 4 * g + j
                    last = mm(ps[32 * j:32 * j + 32, 6 * QW:7 * QW], v_sb[:, kt * VW:kt * VW + VW],
                              p_ring[:, kt % 8, :],
                              start=g == 0, stop=g == GROUPS - 1)
                last.then_inc(pv_done, 1)

            def turn_outputs(it):
                pe.wait_ge(o_evac, it + 2)
                for qt in range(TPB):
                    last = tr(ps[:, 7 * QW + qt * P:7 * QW + qt * P + P], o_sb[:, qt * P:qt * P + P], ident)
                last.then_inc(o_turned, 1)

            def attention_pair(b, peeled=None):
                snap = pe.snap if peeled is None else (lambda v: v)
                qc, kc = snap((b % QRING) * QW), snap(((b >> 3) % 3) * T)
                qn, kn = snap(((b + 2) % QRING) * QW), snap((((b + 2) >> 3) % 3) * T)
                e0, u0 = snap(b * EXPS), snap((b + 2) * UNITS)
                for o in (0, 1):
                    attention_step(b + o, qc + o * QW, kc, qn + o * QW, kn, e0 + o * EXPS, u0 + o * UNITS,
                                   prev=peeled is None or b + o > 0, scores=peeled is None or b + o + 2 < STEPS,
                                   maxima=peeled is None or b + o + 1 < STEPS)

            def attention_step(it, qc, kc, qn, kn, e0, u0, prev, scores, maxima):
                if scores:
                    pe.wait_ge(q_in, 96 * (it + 3))
                    pe.wait_ge(k_in, (((it + 2) >> 3) + 1) * (96 * NQ))

                def keys(kt):
                    pe.wait_ge(exp_done, e0 + freed(kt))
                    mm(bank(kt % RING), k_ring[0:NAUG, ds(kc + kt * P, P)], q_ring[0:NAUG, ds(qc, QW)],
                       start=True, stop=True).then_inc(st_ready, 1)

                def unit(u):
                    if scores:
                        score_unit(u, u0, qn, kn)

                for s in range(GROUPS):
                    if s >= PV_LAG:
                        pv_group(it, e0, s - PV_LAG)
                    elif prev:
                        pv_group(it - 1, e0 - EXPS, s - PV_LAG + GROUPS)
                    for j in range(3):
                        unit(4 * s + j)
                        if s == 0 and j == 0:
                            pe.wait_ge(mrow_ready, it + 1)
                        keys(4 * s + j)
                    if s == 3 and prev:
                        turn_outputs(it - 1)
                    if s == 5 and maxima:
                        if prev:
                            pe.wait_ge(osum_ready, it)
                        transpose_maxima(it + 1)
                    unit(4 * s + 3)
                    keys(4 * s + 3)

            attention_pair(0, peeled=True)
            with pe.Fori(1, STEPS // 2 - 1) as i:
                attention_pair(i * 2)
            attention_pair(STEPS - 2, peeled=True)
            for g in range(GROUPS - PV_LAG, GROUPS):
                pv_group(STEPS - 1, (STEPS - 1) * EXPS, g)
            pe.wait_ge(osum_ready, STEPS - 1)
            turn_outputs(STEPS - 1)

            wo3 = wout[:].rearrange("p (k c) -> p k c", k=KC)
            wg3 = wgate[:].rearrange("p (k c) -> p k c", k=KC)
            pe.wait_ge(vec_in, 64)

            def turn(c, i, par):
                pe.wait_ge(at_in[par], 16 * (i + 1))
                pe.wait_ge(atT_copied, c + 1)
                for k in range(KC):
                    for t in range(TPB):
                        last = tr(bank(k)[:, t * P:t * P + P], at[par][:, t, k * P:k * P + P], ident)
                last.then_inc(at_tr, 1)

            def project(c, par):
                pe.wait_ge(atT_copied, c + 2)
                pe.wait_ge(x2_chain, 2 * c + 2)
                for b in range(2):
                    for t in (2 * b, 2 * b + 1):
                        for k in range(KC):
                            last = mm(bank(2 + b)[:, (t % 2) * D:(t % 2) * D + D], atT[par][:, k * QW + t * P:k * QW + t * P + P],
                                      wo3[:, k, :], start=k == 0, stop=k == KC - 1)
                    last.then_inc(proj2_ready, 1)

            def turn_normed(c, par):
                pe.wait_ge(xs_ready, c + 1)
                pe.wait_ge(xsT_copied, c + 1)
                for k in range(KC):
                    for t in range(TPB):
                        last = tr(bank(4 + k)[:, t * P:t * P + P], xs[par][:, t, k * P:k * P + P], ident)
                last.then_inc(xs_tr, 1)

            def gate(c, par):
                pe.wait_ge(xsT_copied, c + 2)
                pe.wait_ge(gate_read, c + 1)
                for t in range(TPB):
                    for k in range(KC):
                        last = mm(bank(6)[:, t * E:t * E + E], xsT[par][:, k * QW + t * P:k * QW + t * P + P], wg3[:, k, :],
                                  start=k == 0, stop=k == KC - 1)
                last.then_inc(gate_ready, 1)

            def chunk_step(c, i, par, more=True):
                project(c, par)
                turn_normed(c - 1, 1 - par)
                if more:
                    turn(c + 1, i + par, 1 - par)
                gate(c - 1, 1 - par)

            turn(0, 0, 0)
            project(0, 0)
            turn(1, 0, 1)
            with pe.Fori(0, NQ // 2 - 1) as i:
                chunk_step(i * 2 + 1, i, 1)
                chunk_step(i * 2 + 2, i + 1, 0)
            chunk_step(NQ - 1, NQ // 2 - 1, 1, more=False)
            turn_normed(NQ - 1, 1)
            gate(NQ - 1, 1)

            pe.wait_ge(rank_in, 1)
            mm(bank(4)[:, 0:NT * E], trib[:], maskb, start=True, stop=True)
            mm(bank(5)[:, 0:NT * E], onesb[:], maskb, start=True, stop=True).then_inc(rank_out, 1)

            def turn_slots(e, i, par):
                pe.wait_ge(xin_in[par], 16 * (i + 1))
                pe.wait_ge(xi_lo, e + 1)
                pe.wait_ge(xi_mid, e + 1)
                pe.wait_ge(xi_hi, e + 1)
                for k in range(KC):
                    for s in range(ST):
                        o = (k * ST + s) * P
                        last = tr(ps[:, o:o + P], xin[par][:, s, k * P:k * P + P], ident)
                last.then_inc(xi_tr, 1)

            def layer1(e, i, par):
                pe.wait_ge(we_in[par], 64 * (i + 1))
                pe.wait_ge(xi_lo, e + 2)
                pe.wait_ge(xi_mid, e + 2)
                pe.wait_ge(xi_hi, e + 2)
                for f in range(FT):
                    done = h_act if f % 2 == 0 else h_dve
                    pe.wait_ge(done, FT // 2 * e + f // 2 + 1)
                    for hf in range(2):
                        for k in range(KC):
                            o = k * CAP + hf * CAP // 2
                            last = mm(bank(3 + 2 * (f % 2) + hf)[:, 0:CAP // 2], w1s[par][:, k, f * P:f * P + P],
                                      xinT[par][:, o:o + CAP // 2], start=k == 0, stop=k == KC - 1)
                    last.then_inc(h_ready, 1)

            def layer2(e, par):
                pe.wait_ge(h_act, FT // 2 * e + FT // 2 + 1)
                pe.wait_ge(h_dve, FT // 2 * e + FT // 2 + 1)
                for s in range(ST):
                    pe.wait_ge(y_read, ST * e + s + 1)
                    for f in range(FT):
                        last = mm(y_bank(e, par, s), hT[:, f, s * P:s * P + P], w2s[par][:, f, :],
                                  start=f == 0, stop=f == FT - 1)
                    last.then_inc(y_ready, 1)

            def y_bank(e, par, s):
                return bank(7)[:, 0:D] if (s + par) % 2 == 0 else bank(2)[:, D:2 * D]

            def expert(e, i, par, more):
                layer1(e, i, par)
                if more:
                    turn_slots(e + 1, i + par, 1 - par)
                    pe.wait_ge(xi_hi, e + 3)
                layer2(e, par)

            turn_slots(0, 0, 0)
            with pe.Fori(0, E // 2 - 1) as i:
                for par in (0, 1):
                    expert(i * 2 + par, i, par, True)
            expert(E - 2, E // 2 - 1, 0, True)
            expert(E - 1, E // 2 - 1, 1, False)

        @block.scalar
        def _(act):
            av = nc.scalar.activation
            act.sem_inc(xt_lo, 1)
            act.sem_inc(proj_read, 4)
            act.sem_inc(exp_done, RING)
            act.sem_inc(o_evac, 1)
            act.wait_ge(consts_ready, 3)

            def deviation(n, width):
                act.wait_ge(var_ready, n + 1)
                av(dev[:, 0:width], mv[:].rearrange("p (t s) -> p t s", s=2)[:, 0:width, 1], ACT.Sqrt,
                   bias=eps[:, 0:1]).then_inc(dev_ready, 1)

            def copy_turned(c, par):
                act.wait_ge(xt_ready, 2 * c + 1)
                av(xnT[par][:, 0, :], bank(0), ACT.Copy).then_inc(xt_lo, 1)

            def project_chunk(c, i, par):
                act.wait_ge(parts_out[par], 12 * 16 * (i + 1))
                for f in range(4):
                    act.wait_ge(proj_ready, 4 * c + f + 1)
                    if f < 2:
                        act.wait_ge(split_v, 2 * c + f + 1)
                    else:
                        act.wait_ge(split_p, 2 * c + f - 1)
                    scale = SCALE if f < 2 else 1.0
                    av(xf[:, f, :], bank(2 + f), ACT.Identity, bias=bqk[:, f:f + 1], scale=scale)
                    av(parts[par][:, f, 0, :], bank(2 + f), ACT.Identity, bias=bqk[:, f:f + 1],
                       scale=scale).then_inc(proj_read, 1)

            def chunk_step(c, i, par):
                deviation(c + 1, TPB)
                project_chunk(c, i, par)
                copy_turned(c + 1, 1 - par)

            deviation(0, TPB)
            copy_turned(0, 0)
            with act.Fori(0, NQ // 2 - 1) as i:
                for par in (0, 1):
                    chunk_step(i * 2 + par, i, par)
            chunk_step(NQ - 2, NQ // 2 - 1, 0)
            project_chunk(NQ - 1, NQ // 2 - 1, 1)

            def copy_maxima(j):
                act.wait_ge(mt_ready, j + 1)
                av(q_ring[NPR:NAUG, ds((j % QRING) * QW, QW)], ps[NPR:NAUG, 7 * QW:8 * QW], ACT.Copy).then_inc(mrow_ready, 1)

            for par in (0, 1):
                act.wait_ge(parts_out[par], 12 * 16 * (NQ // 2 + 1))
            copy_maxima(0)

            def evacuate(it):
                act.wait_ge(pv_done, GROUPS * it + GROUPS + 2)
                act.wait_ge(o_turned, it + 1)
                av(o_sb[:], bank(6), ACT.Copy).then_inc(o_evac, 1)

            def attention_step(it, prev=True, maxima=True):
                snap = (lambda v: v) if isinstance(it, int) else act.snap
                e0, g0 = snap(it * EXPS), snap(it * GROUPS)
                for n in range(EXPS):
                    act.wait_ge(st_ready, e0 + n + 1)
                    act.wait_ge(pv_done, g0 + n // 4 + 1)
                    av(p_ring[:, n % 8, :], bank(n % RING), ACT.Exp).then_inc(exp_done, 1)
                    if n == 4 * (PV_LAG - 1) - 1 and prev:
                        evacuate(it - 1)
                    if n == 25 and maxima:
                        copy_maxima(it + 1)

            attention_step(0, prev=False)
            with act.Fori(1, STEPS - 1) as it:
                attention_step(it)
            attention_step(STEPS - 1, maxima=False)
            evacuate(STEPS - 1)

            def copy_rows(c, par):
                act.wait_ge(at_tr, c + 3)
                av(atT[par], bank(0, 2), ACT.Copy).then_inc(atT_copied, 1)

            def copy_normed(c, par):
                act.wait_ge(xs_tr, c + 1)
                av(xsT[par], bank(4, 2), ACT.Copy).then_inc(xsT_copied, 1)

            def chunk_copies(c, par, more=True):
                copy_normed(c - 1, 1 - par)
                if more:
                    copy_rows(c + 1, 1 - par)
                deviation(NQ + c, TPB)

            act.sem_inc(atT_copied, 1)
            act.sem_inc(xsT_copied, 1)
            copy_rows(0, 0)
            copy_rows(1, 1)
            deviation(NQ, TPB)
            with act.Fori(0, NQ // 2 - 1) as i:
                chunk_copies(i * 2 + 1, 1)
                chunk_copies(i * 2 + 2, 0)
            chunk_copies(NQ - 1, 1, more=False)
            copy_normed(NQ - 1, 1)

            act.wait_ge(exp_in, 1)
            av(rt[2], rt[1], ACT.Exp).then_inc(exp_out, 1)

            act.sem_inc(xi_lo, 1)
            act.sem_inc(h_act, 1)

            def slots_copy(e, par):
                act.wait_ge(xi_tr, e + 1)
                av(xinT[par][:, 0:QW], bank(0), ACT.Copy).then_inc(xi_lo, 1)

            def expert(e, i, par, more):
                act.wait_ge(we_in[par], 64 * (i + 1))
                for f in range(0, FT, 2):
                    act.wait_ge(h_ready, FT * e + f + 1)
                    av(hT[:, f, :].rearrange("p (a c) -> p a c", a=2),
                       bank(3, 2).rearrange("p (a c) -> p a c", a=2)[:, :, 0:CAP // 2], ACT.Relu,
                       bias=b1s[:, FT * par + f:FT * par + f + 1]).then_inc(h_act, 1)
                if more:
                    slots_copy(e + 1, 1 - par)

            slots_copy(0, 0)
            with act.Fori(0, E // 2 - 1) as i:
                for par in (0, 1):
                    expert(i * 2 + par, i, par, True)
            expert(E - 2, E // 2 - 1, 0, True)
            expert(E - 1, E // 2 - 1, 1, False)

        @block.gpsimd
        def _(pool):
            g = nc.gpsimd
            pool.sem_inc(split_p, 2)
            g.memset(zeros[:], 0.0).then_inc(zeros_ready, 1)
            for par in (0, 1):
                g.memset(vst[par][:, :, :, HD:VW], 0.0).then_inc(vst_ready, 1)
                pool.wait_ge(vst_ready, 2 * par + 1)
                g.memset(vst[par][:, :, :, HD:HD + 1], 1.0).then_inc(vst_ready, 1)
            pool.wait_ge(vst_ready, 4)
            g.memset(k_ring[NPR:NAUG, :], 1.0).then_inc(ring_ones, 1)

            pool.wait_ge(ring_ones, 1)

            def split_chunk(c, par):
                link = chain(pool, chain_p, c * 4)
                for f in (2, 3):
                    pool.wait_ge(proj_read, 4 * c + f + 5)
                    link(g.tensor_tensor(res[:, 1, :], xf[:, f, :], parts[par][:, f, 0, :], ALU.subtract))
                    link(g.tensor_copy(parts[par][:, f, 1, :], res[:, 1, :]))
                    g.tensor_tensor(parts[par][:, f, 2, :], res[:, 1, :], parts[par][:, f, 1, :], ALU.subtract).then_inc(split_p, 1)
                    pool.wait_ge(split_p, 2 * c + f + 1)

            with pool.Fori(0, NQ // 2) as i:
                for par in (0, 1):
                    split_chunk(i * 2 + par, par)

            msp = msplit[:].rearrange("p (t n) -> p n t", n=4)

            def split_maxima(j):
                link = chain(pool, split_chain, j * 4)
                pool.wait_ge(mx_ready, j + 1)
                if not isinstance(j, int) or j > 0:
                    pool.wait_ge(mt_ready, j)
                lone_wait(pool)
                link(g.tensor_scalar(mneg[:], mx[:], -1.0, None, ALU.mult))
                link(g.tensor_copy(msp[:, 0, :], mneg[:]))
                link(g.tensor_tensor(mres[:], mneg[:], msp[:, 0, :], ALU.subtract))
                link(g.tensor_copy(msp[:, 1, :], mres[:]))
                g.tensor_tensor(msp[:, 2, :], mres[:], msp[:, 1, :], ALU.subtract).then_inc(msplit_ready, 1)

            split_maxima(0)
            pool.wait_ge(vec_in, 64)
            pool.wait_ge(ln_ready, NQ)
            with pool.Fori(0, NQ) as c:
                four = x_all[:, ds(c * TPB * D, TPB * D)].rearrange("p (t c) -> p t c", t=TPB)
                g.tensor_tensor(four, four, bout[:].unsqueeze(1).to_broadcast([P, TPB, D]), ALU.add).then_inc(x_biased, 1)
            with pool.Fori(1, STEPS) as j:
                split_maxima(j)

            pool.sem_inc(xs_kept, 2)
            with pool.Fori(0, NQ // 2) as i:
                for par in (0, 1):
                    c = i * 2 + par
                    pool.wait_ge(xs_ready, c + 1)
                    lone_wait(pool)
                    g.tensor_copy(a_all[:, ds(c * TPB * D, TPB * D)], xs[par].rearrange("p t c -> p (t c)")).then_inc(xs_kept, 1)
            pool.wait_ge(xs_kept, NQ + 2)

            pool.wait_ge(zero_out, 16 * (E * CAP // (2 * P)))
            pool.wait_ge(slots_ready, 2)
            for t in range(NT):
                for j in range(2):
                    g.indirect_dma_start(xin_d, bass.IndirectOffsetOnAxis(slot_w[:, j * NT + t:j * NT + t + 1], 0),
                                         a_t[:, t, :], None, bounds_check=E * CAP - 1, oob_is_err=False).then_inc(scattered, 16)
            pool.wait_ge(y_out[0], 16 * (E // 2 + 1))
            pool.wait_ge(y_out[1], 16 * (E // 2 + 1))
            for t in range(NT):
                if t >= G:
                    pool.wait_ge(o_ready, t - G + 1)
                for j in range(2):
                    g.indirect_dma_start(gat[t % G][j], None, y_d,
                                         bass.IndirectOffsetOnAxis(slot_r[:, j * NT + t:j * NT + t + 1], 0)).then_inc(g_in[t % G], 16)

        @block.vector
        def _(dve):
            v = nc.vector
            dve.sem_inc(xt_hi, 1)
            dve.sem_inc(v_evac, 2)
            dve.sem_inc(split_v, 2)
            dve.sem_inc(max_done, RING)
            dve.wait_ge(const_in, 16)
            dve.wait_ge(w_in, 48)
            v.tensor_scalar(bqk[:, 0:2], bqk[:, 0:2], SCALE, None, ALU.mult).then_inc(consts_ready, 1)
            v.tensor_copy(identb[:], ident)
            v.tensor_copy(trib[:], cst[:, P:2 * P]).then_inc(consts_ready, 1)
            v.memset(eps[:], EPS)
            v.memset(onesb[:], 1.0).then_inc(consts_ready, 1)
            dve.wait_ge(vst_ready, 4)

            st3 = stats[:].rearrange("p (t s) -> p t s", s=6)
            mv3 = mv[:].rearrange("p (t s) -> p t s", s=2)

            def normalise(c, par):
                link = chain(dve, ln_chain, c * 1)
                dve.wait_ge(x_in, 16 * (c + 1))
                lone_wait(dve)
                for t in range(TPB):
                    last = v.bn_stats(st3[:, t, :], x_all[:, ds((c * TPB + t) * D, D)])
                link(last)
                for t in range(TPB):
                    last = v.bn_aggr(mv3[:, t, :], st3[:, t, :])
                last.then_inc(var_ready, 1)
                dve.wait_ge(dev_ready, c + 1)
                v.reciprocal(rstd[:], dev[:]).then_inc(rstd_ready, 1)
                dve.wait_ge(rstd_ready, c + 1)
                for t in range(TPB):
                    last = v.tensor_scalar(xn[par][:, t, :], x_all[:, ds((c * TPB + t) * D, D)], mv3[:, t, 0:1],
                                           rstd[:, t:t + 1], ALU.subtract, ALU.mult)
                last.then_inc(ln_ready, 1)

            def copy_turned(c, par):
                dve.wait_ge(xt_ready, 2 * c + 2)
                v.tensor_copy(xnT[par][:, 1, :], bank(1)).then_inc(xt_hi, 1)

            def split_queries(c, par):
                link = Chain(dve, chain_v, c * 4)
                for f in (0, 1):
                    dve.wait_ge(proj_read, 4 * c + f + 5)
                    link(v.tensor_tensor(res[:, 0, :], xf[:, f, :], parts[par][:, f, 0, :], ALU.subtract))
                    link(v.tensor_copy(parts[par][:, f, 1, :], res[:, 0, :]))
                    v.tensor_tensor(parts[par][:, f, 2, :], res[:, 0, :], parts[par][:, f, 1, :], ALU.subtract).then_inc(split_v, 1)
                    dve.wait_ge(split_v, 2 * c + f + 3)

            def take_values(c, i, par):
                dve.wait_ge(v_out[par], 16 * (i + 1))
                for b in range(2):
                    dve.wait_ge(v_ready, 2 * c + b + 1)
                    for t in range(2):
                        last = v.tensor_tensor(vst[par][:, :, 2 * b + t, 0:HD],
                                               bank(6 + b)[:, t * D:t * D + D].rearrange("p (h c) -> p h c", h=H),
                                               bv[:].rearrange("p (h c) -> p h c", h=H), ALU.add)
                    last.then_inc(v_evac, 1)

            def chunk_step(c, i, par, more=True):
                if more:
                    normalise(c + 1, 1 - par)
                split_queries(c, par)
                if more:
                    copy_turned(c + 1, 1 - par)
                take_values(c, i, par)

            normalise(0, 0)
            copy_turned(0, 0)
            with dve.Fori(0, NQ // 2 - 1) as i:
                for par in (0, 1):
                    chunk_step(i * 2 + par, i, par)
            chunk_step(NQ - 2, NQ // 2 - 1, 0)
            chunk_step(NQ - 1, NQ // 2 - 1, 1, more=False)

            groups = bank(7).rearrange("p (t g c) -> p t c g", t=TPB, g=4)[:, :, 0:HD + 1, :]
            sums = osum[:].rearrange("p (t c) -> p t c", t=TPB)

            def maximum(u, base, par):
                dve.wait_ge(s_ready, base + u + 1)
                v.tensor_reduce(mpart[:, UNITS * par + u:UNITS * par + u + 1], bank(RING + u % RING), AX.X,
                                ALU.max).then_inc(max_done, 1)

            def reduce_maxima(j, par):
                dve.wait_ge(max_done, (j + 1) * UNITS + RING)
                if not isinstance(j, int) or j > 0:
                    dve.wait_ge(msplit_ready, j)
                v.tensor_reduce(mx[:], mpart[:, UNITS * par:UNITS * par + UNITS].rearrange("p (t c) -> p t c", t=TPB),
                                AX.X, ALU.max).then_inc(mx_ready, 1)

            def sum_groups(it):
                if not isinstance(it, int) or it > 0:
                    dve.wait_ge(rows_ready, it)
                dve.wait_ge(o_turned, it + 2)
                v.tensor_reduce(sums, groups, AX.X, ALU.add).then_inc(osum_ready, 1)

            def invert_sums(it):
                dve.wait_ge(osum_ready, it + 1)
                v.reciprocal(rden[:], sums[:, :, HD]).then_inc(rden_ready, 1)

            def write_rows(it):
                dve.wait_ge(rows_out, 16 * (it + 1))
                dve.wait_ge(rden_ready, it + 1)
                v.tensor_tensor(rows[:, ds((it % 2) * TPB * HD, TPB * HD)].rearrange("p (t c) -> p t c", c=HD),
                                sums[:, :, 0:HD], rden[:].unsqueeze(2).to_broadcast([P, TPB, HD]),
                                ALU.mult).then_inc(rows_ready, 1)

            for j in (0, 1):
                for u in range(UNITS):
                    maximum(u, UNITS * j, j)
                    if u == 1 and j == 1:
                        reduce_maxima(0, 0)

            def attention_step(it, par, u0, prev=True, scores=True, maxima=True):
                dve.wait_ge(mx_ready, it + 1)
                for u in range(UNITS):
                    if scores:
                        maximum(u, u0, par)
                    if u == 1 and maxima:
                        reduce_maxima(it + 1, 1 - par)
                    if prev:
                        if u == 17:
                            sum_groups(it - 1)
                        if u == 18:
                            invert_sums(it - 1)
                        if u == 19:
                            write_rows(it - 1)

            attention_step(0, 0, 2 * UNITS, prev=False)
            attention_step(1, 1, 3 * UNITS)
            with dve.Fori(1, STEPS // 2 - 1) as i:
                u0 = dve.snap((i * 2 + 2) * UNITS)
                for o in (0, 1):
                    attention_step(i * 2 + o, o, u0 + o * UNITS)
            attention_step(STEPS - 2, 0, 0, scores=False)
            attention_step(STEPS - 1, 1, 0, scores=False, maxima=False)
            sum_groups(STEPS - 1)
            invert_sums(STEPS - 1)
            write_rows(STEPS - 1)

            dve.wait_ge(vec_in, 64)
            dve.wait_ge(x_biased, NQ)
            dve.sem_inc(x2_chain, 2)
            logits = rt[0]

            def residual(c, par):
                for b in range(2):
                    dve.wait_ge(proj2_ready, 2 * c + b + 1)
                    two = x_all[:, ds((c * TPB + 2 * b) * D, 2 * D)]
                    v.tensor_tensor(two, bank(2 + b), two, ALU.add).then_inc(x2_chain, 1)
                link = chain(dve, ln_chain, c + NQ)
                dve.wait_ge(x2_chain, 2 * c + 4)
                lone_wait(dve)
                for t in range(TPB):
                    last = v.bn_stats(st3[:, t, :], x_all[:, ds((c * TPB + t) * D, D)])
                link(last)
                for t in range(TPB):
                    last = v.bn_aggr(mv3[:, t, :], st3[:, t, :])
                last.then_inc(var_ready, 1)
                dve.wait_ge(dev_ready, NQ + c + 1)
                v.reciprocal(rstd[:], dev[:]).then_inc(rstd_ready, 1)
                dve.wait_ge(xs_kept, c + 1)
                dve.wait_ge(rstd_ready, NQ + c + 1)
                for t in range(TPB):
                    last = v.tensor_scalar(xs[par][:, t, :], x_all[:, ds((c * TPB + t) * D, D)], mv3[:, t, 0:1],
                                           rstd[:, t:t + 1], ALU.subtract, ALU.mult)
                last.then_inc(xs_ready, 1)

            def read_gate(c):
                dve.wait_ge(gate_ready, c + 1)
                v.tensor_tensor(arena[:, ds(c * TPB * E, TPB * E)].rearrange("p (t e) -> p t e", e=E),
                                bank(6)[:, 0:TPB * E].rearrange("p (t e) -> p t e", e=E),
                                bgate[:].unsqueeze(1).to_broadcast([P, TPB, E]), ALU.add).then_inc(gate_read, 1)

            dve.sem_inc(gate_read, 1)
            dve.wait_ge(q_in, 96 * (STEPS + Q_AHEAD))
            dve.wait_ge(k_in, 96 * (STEPS + K_AHEAD))
            residual(0, 0)
            with dve.Fori(0, NQ // 2 - 1) as i:
                for par in (1, 0):
                    c = i * 2 + (1 if par else 2)
                    residual(c, par)
                    read_gate(c - 1)
            residual(NQ - 1, 1)
            read_gate(NQ - 2)
            read_gate(NQ - 1)
            dve.wait_ge(gate_read, NQ + 1)

            link = Chain(dve, route_chain)

            def wide(a):
                return a.unsqueeze(2).to_broadcast([P, NT, E])

            ex = iota_e.unsqueeze(1).to_broadcast([P, NT, E])
            rmax, rsum, rrec = r1[0], r1[1], r1[2]
            link(v.tensor_reduce(rmax, logits, AX.X, ALU.max))
            v.tensor_tensor(rt[1], logits, wide(rmax), ALU.subtract).then_inc(exp_in, 1)
            dve.wait_ge(exp_out, 1)
            link(v.tensor_reduce(rsum, rt[2], AX.X, ALU.add))
            link(v.reciprocal(rrec, rsum))
            link(v.tensor_tensor(rt[3], rt[2], wide(rrec), ALU.mult))
            prob = rt[3]
            sel = []
            for n in range(2):
                top, idx = r1[3 + n], r1[5 + n]
                link(v.tensor_reduce(top, prob, AX.X, ALU.max))
                link(v.tensor_tensor(rt[4], prob, wide(top), ALU.is_lt))
                link(v.scalar_tensor_tensor(rt[5], rt[4], float(E), ex, ALU.mult, ALU.add))
                link(v.tensor_reduce(idx, rt[5], AX.X, ALU.min))
                pick = rt[6 + n]
                link(v.tensor_tensor(pick, ex, wide(idx), ALU.is_equal))
                sel.append(pick)
                if n == 0:
                    link(v.scalar_tensor_tensor(rt[8], pick, -2.0, prob, ALU.mult, ALU.add))
                    prob = rt[8]
            v.tensor_tensor(maskb.rearrange("p (t e) -> p t e", e=E), sel[0], sel[1], ALU.add).then_inc(rank_in, 1)
            dve.wait_ge(rank_out, 1)
            tot = [rt[9], rt[10]]
            link(v.tensor_copy(tot[0], bank(5)[:, 0:NT * E].rearrange("p (t e) -> p t e", e=E)))
            cur, step = 0, 1
            while step < NT:
                a, b = tot[cur], tot[1 - cur]
                link(v.tensor_copy(b[:, 0:step, :], a[:, 0:step, :]))
                link(v.tensor_tensor(b[:, step:NT, :], a[:, step:NT, :], a[:, 0:NT - step, :], ALU.add))
                cur, step = 1 - cur, 2 * step
            rank, slot = rt[11], rt[12]
            link(v.tensor_copy(rank, bank(4)[:, 0:NT * E].rearrange("p (t e) -> p t e", e=E)))
            link(v.tensor_tensor(rank[:, 1:NT, :], rank[:, 1:NT, :], tot[cur][:, 0:NT - 1, :], ALU.add))
            over = rt[13]
            link(v.tensor_scalar(over, rank, float(CAP), None, ALU.is_gt))
            link(v.tensor_tensor(slot, rank, slot_base.unsqueeze(1).to_broadcast([P, NT, E]), ALU.add))
            den = r1[7]
            link(v.tensor_tensor(den, r1[3], r1[4], ALU.add))
            link(v.reciprocal(den, den))
            for n in range(2):
                s_n, o_n, f_n = r1[8 + n], r1[10 + n], r1[12 + n]
                link(v.tensor_tensor(rt[14], sel[n], slot, ALU.mult))
                link(v.tensor_reduce(s_n, rt[14], AX.X, ALU.add))
                link(v.tensor_tensor(rt[15], sel[n], over, ALU.mult))
                link(v.tensor_reduce(o_n, rt[15], AX.X, ALU.add))
                link(v.scalar_tensor_tensor(f_n, o_n, BIG, s_n, ALU.mult, ALU.add))
                link(v.tensor_copy(slot_w[:, n * NT:n * NT + NT], f_n))
                link(v.tensor_scalar(s_n, s_n, float(E * CAP - 1), None, ALU.min))
                link(v.tensor_copy(slot_r[:, n * NT:n * NT + NT], s_n))
                link(v.tensor_scalar(o_n, o_n, -1.0, 1.0, ALU.mult, ALU.add))
                link(v.tensor_tensor(f_n, r1[3 + n], den, ALU.mult))
                v.tensor_tensor(wgt[:, n * NT:n * NT + NT], f_n, o_n, ALU.mult).then_inc(slots_ready, 1)

            dve.sem_inc(xi_mid, 1)
            dve.sem_inc(xi_hi, 1)
            dve.sem_inc(h_dve, 1)
            dve.sem_inc(y_read, 2)

            def slots_copy(e, par):
                dve.wait_ge(xi_tr, e + 1)
                v.tensor_copy(xinT[par][:, QW:2 * QW], bank(1)).then_inc(xi_mid, 1)
                v.tensor_copy(xinT[par][:, 2 * QW:2 * CAP], bank(2)[:, 0:2 * CAP - 2 * QW]).then_inc(xi_hi, 1)

            def expert(e, i, par, more):
                dve.wait_ge(we_in[par], 64 * (i + 1))
                for f in range(1, FT, 2):
                    dve.wait_ge(h_ready, FT * e + f + 1)
                    v.tensor_scalar(hT[:, f, :].rearrange("p (a c) -> p a c", a=2),
                                    bank(5, 2).rearrange("p (a c) -> p a c", a=2)[:, :, 0:CAP // 2],
                                    b1s[:, FT * par + f:FT * par + f + 1], 0.0, ALU.add, ALU.max).then_inc(h_dve, 1)
                if more:
                    slots_copy(e + 1, 1 - par)
                dve.wait_ge(y_out[par], 16 * (i + 1))
                for s in range(ST):
                    src = bank(7)[:, 0:D] if (s + par) % 2 == 0 else bank(2)[:, D:2 * D]
                    dve.wait_ge(y_ready, ST * e + s + 1)
                    v.tensor_tensor(ys[par][:, s, :], src, b2s[:, D * par:D * par + D], ALU.add).then_inc(y_read, 1)

            slots_copy(0, 0)
            with dve.Fori(0, E // 2 - 1) as i:
                for par in (0, 1):
                    expert(i * 2 + par, i, par, True)
            expert(E - 2, E // 2 - 1, 0, True)
            expert(E - 1, E // 2 - 1, 1, False)

            for t in range(NT):
                dve.wait_ge(g_in[t % G], 32 * (t // G + 1))
                v.scalar_tensor_tensor(x_t[:, t, :], gat[t % G][0], wgt[:, t:t + 1], x_t[:, t, :],
                                       ALU.mult, ALU.add).then_inc(o_chain, 1)
                dve.wait_ge(o_chain, t + 1)
                v.scalar_tensor_tensor(x_t[:, t, :], gat[t % G][1], wgt[:, NT + t:NT + t + 1], x_t[:, t, :],
                                       ALU.mult, ALU.add).then_inc(o_ready, 1)


INPUTS = ["L0_attn_x", "L0_attn_W_qkv", "L0_attn_b_qkv", "L0_attn_W_out", "L0_attn_b_out", "L0_ffn_gate_w",
          "L0_ffn_gate_b", "L0_ffn_w1", "L0_ffn_b1", "L0_ffn_w2", "L0_ffn_b2"]


def constants():
    c = np.zeros((P, CW), np.float32)
    c[:, 0:P] = np.eye(P)
    c[:, P:2 * P] = np.triu(np.ones((P, P)))
    c[:, 2 * P:2 * P + E] = np.arange(E)
    c[:, 2 * P + E:] = np.arange(E) * CAP - 1
    return c


def kernel(**inputs):
    import concourse.bacc as bacc
    from concourse.bass_utils import run_bass_kernel_spmd

    nc = bacc.Bacc("TRN2", target_bir_lowering=False, num_devices=1)
    arrays = {name: np.ascontiguousarray(inputs[name]) for name in INPUTS}
    arrays["consts"] = constants()
    aps = [nc.dram_tensor(n, a.shape, mybir.dt.from_np(a.dtype), kind="ExternalInput").ap() for n, a in arrays.items()]
    out = nc.dram_tensor("out", (1, T, D), F32, kind="ExternalOutput").ap()
    build(nc, *aps, out)
    r = run_bass_kernel_spmd(nc, [arrays], core_ids=[0])
    return r.results[0]["out"]
```

```python
from contextlib import ExitStack

import numpy as np

import concourse.bass as bass
from concourse import mybir

F32 = mybir.dt.float32
BF16 = mybir.dt.bfloat16
U32 = mybir.dt.uint32
ALU = mybir.AluOpType
ACT = mybir.ActivationFunctionType
AX = mybir.AxisListType
ds = bass.ds

P = 128
T, D, H, HD = 4096, 256, 16, 16
NT = T // P
QW = 512
NQ = T // QW
TPB = QW // P
STEPS = H * NQ
NCH = T // QW
E, FF = 8, 1024
CAP = int(1.25 * T / E)
ST = CAP // P
KC = D // P
FT = FF // P
EPS = 1e-5
SCALE = 1.0 / float(np.sqrt(HD))
Q_PARTS = (0, 1, 2, 0, 1, 0)
K_PARTS = (0, 0, 0, 1, 1, 2)
NPR = 16 * len(Q_PARTS)
LOADED = 16 * len(Q_PARTS)
PARTS_STORED = 16 * 4
NAUG = NPR + 3
QRING, KRING = 16, 24
Q_AHEAD, K_AHEAD = 4, 12
VW = 32
EXPS = T // P
UNITS = TPB * NCH
RING = 3
GROUPS = T // (4 * P)
PV_LAG = 2
BIG = 1.0e6
NS = E * ST
NC = 2 * NT
CW = P + P + E + E + P + NS + NC + 1


def freed(n):
    assert EXPS % RING == 2 and UNITS % RING == 2
    return n + 1 if n >= 2 else n + 2


class Chain:

    def __init__(self, eng, sem, base=0):
        self.eng, self.sem, self.n = eng, sem, base

    def __call__(self, ins):
        ins.then_inc(self.sem, 1)
        self.n = self.n + 1
        self.eng.wait_ge(self.sem, self.n)


def build(nc, x, w_qkv, b_qkv, w_out, b_out, gate_w, gate_b, w1, b1, w2, b2, consts, out):
    qk_d = nc.dram_tensor("qk_parts", (2, 3, D, T), BF16, kind="Internal").ap()
    v_d = nc.dram_tensor("v_heads", (H, P, NT * VW), F32, kind="Internal").ap()
    att_d = nc.dram_tensor("attention_rows", (STEPS * QW, HD), F32, kind="Internal").ap()
    xn2_d = nc.dram_tensor("normed_rows", (T, D), F32, kind="Internal").ap()
    y_d = nc.dram_tensor("expert_out", (2 * T, D), F32, kind="Internal").ap()

    with ExitStack() as ctx:
        def sb(name, cols, dt=F32):
            return ctx.enter_context(nc.sbuf_tensor(name, [P, cols], dt))

        def sem(name):
            return ctx.enter_context(nc.semaphore(name))

        cst = sb("cst", CW)
        ident = cst[:, 0:P]
        iota_e = cst[:, 2 * P:2 * P + E]
        slot_base = cst[:, 2 * P + E:2 * P + 2 * E]
        o = 2 * P + 2 * E
        iota_p, iota_s, tile_n, row_n = cst[:, o:o + P], cst[:, o + P:o + P + NS], cst[:, o + P + NS:CW - 1], cst[:, CW - 1:CW]
        identb = sb("identb", P, BF16)
        trib = sb("trib", P, BF16)
        onesb = sb("onesb", P, BF16)
        x_all = sb("x_all", NT * D)
        a_all = sb("a_all", NT * D)
        arena = sb("arena", (KRING + QRING) * QW // 2 + 4096)
        extra = sb("extra", 2048)
        wbuf = sb("wbuf", 8192)
        v_sb = sb("v_sb", NT * VW)
        o_sb = sb("o_sb", QW)
        wqkv = sb("wqkv", KC * 3 * D)
        wout = sb("wout", KC * D)
        wgate = sb("wgate", KC * E)
        bqk = sb("bqk", 4)
        bv = sb("bv", D)
        bout = sb("bout", D)
        bgate = sb("bgate", E)
        b1s = sb("b1s", 2 * FT)
        b2s = sb("b2s", 2 * D)
        stats = sb("stats", TPB * 6)
        mv = sb("mv", TPB * 2)
        rstd = sb("rstd", TPB)
        dev = sb("dev", TPB)
        eps = sb("eps", 1)
        mpart = sb("mpart", 2 * UNITS)
        mx = sb("mx", TPB)
        mneg = sb("mneg", TPB)
        mres = sb("mres", TPB)
        msplit = sb("msplit", TPB * 4, BF16)
        osum = sb("osum", TPB * (HD + 1))
        rden = sb("rden", TPB)
        rows = sb("rows", 2 * TPB * HD)

        x_t = x_all[:].rearrange("p (t c) -> p t c", t=NT)
        kcols, qcols = KRING * QW // 2, QRING * QW // 2
        k_ring = arena[:, 0:kcols].bitcast(BF16)
        q_ring = arena[:, kcols:kcols + qcols].bitcast(BF16)
        p_ring = arena[:, kcols + qcols:kcols + qcols + 4096].rearrange("p (s c) -> p s c", s=8)
        parts = [arena[:, o:o + 3072].bitcast(BF16).rearrange("p (f n c) -> p f n c", f=4, n=3)
                 for o in (kcols, kcols + 3072)]
        res = arena[:, kcols + 6144:kcols + 7168].rearrange("p (s c) -> p s c", s=2)
        vst = [wbuf[:, o:o + 2048].rearrange("p (h t c) -> p h t c", h=H, t=TPB) for o in (0, 2048)]
        xf = wbuf[:, 4096:6144].rearrange("p (f c) -> p f c", f=4)
        xn = [wbuf[:, 6144:7168].rearrange("p (t c) -> p t c", t=TPB),
              wbuf[:, 7168:8192].rearrange("p (t c) -> p t c", t=TPB)]
        xnT = [extra[:, 1024 * i:1024 * i + 1024].rearrange("p (k c) -> p k c", k=KC) for i in (0, 1)]
        at = [a_all[:, 2048 + 1024 * i:3072 + 1024 * i].rearrange("p (t c) -> p t c", t=TPB) for i in (0, 1)]
        atT = [arena[:, 8448 + 1024 * i:9472 + 1024 * i] for i in (0, 1)]
        xs = [arena[:, 10496 + 1024 * i:11520 + 1024 * i].rearrange("p (t c) -> p t c", t=TPB) for i in (0, 1)]
        xsT = [extra[:, 1024 * i:1024 * i + 1024] for i in (0, 1)]
        w1s = [wbuf[:, 4096 * i:4096 * i + 2048].rearrange("p (k f) -> p k f", k=KC) for i in (0, 1)]
        w2s = [wbuf[:, 4096 * i + 2048:4096 * i + 4096].rearrange("p (k c) -> p k c", k=FT) for i in (0, 1)]
        xin = [arena[:, 1280 * i:1280 * i + 1280].rearrange("p (s c) -> p s c", s=ST) for i in (0, 1)]
        xinT = [arena[:, 2560 + 1280 * i:3840 + 1280 * i] for i in (0, 1)]
        ys = [arena[:, 5120 + 1280 * i:6400 + 1280 * i].rearrange("p (s c) -> p s c", s=ST) for i in (0, 1)]
        hT = arena[:, 7680:7680 + FT * CAP].rearrange("p (f c) -> p f c", f=FT)
        rt = [arena[:, 256 * i:256 * i + 256].rearrange("p (t e) -> p t e", e=E) for i in range(20)]
        r1 = [arena[:, 5120 + 32 * i:5152 + 32 * i] for i in range(20)]
        maskb = arena[:, 6144:6272].bitcast(BF16)
        gslot, gcol, gtile = [arena[:, 5760 + NC * i:5760 + NC * i + NC] for i in range(3)]
        gint = arena[:, 5952:5952 + NC].bitcast(U32)
        dec = [arena[:, 4096 + 80 * i:4096 + 80 * i + 2 * NS] for i in range(8)]
        hot_p = a_all[:, 0:4096].bitcast(BF16).rearrange("p (n c) -> p n c", n=NC)
        hot_s = a_all[:, 4096:4096 + NC * NS // 2].bitcast(BF16).rearrange("p (n c) -> p n c", n=NC)
        hot_v = a_all[:, 5376:5376 + NC * NS].bitcast(BF16).rearrange("p (n v c) -> p n v c", n=NC, v=2)
        zeros = a_all[:, 0:2048]
        wgt = sb("wgt", 2 * NT)
        slot_src = sb("slot_src", NS, U32)
        slot_dst = sb("slot_dst", NS, U32)
        yg = [(a_all if i < 8 else arena)[:, 1024 * (i % 8):1024 * (i % 8) + 1024].rearrange("p (t j c) -> p t j c", t=2, j=2)
              for i in range(NT // 2)]

        ps = ctx.enter_context(nc.psum_tensor("ps", [P, 8 * QW], F32))

        def bank(b, n=1):
            return ps[:, b * QW:(b + n) * QW]

        const_in, x_in, w_in, vec_in = sem("const_in"), sem("x_in"), sem("w_in"), sem("vec_in")
        eps_ready = sem("eps_ready")
        consts_ready, zeros_ready, vst_ready = sem("consts_ready"), sem("zeros_ready"), sem("vst_ready")
        zero_out = sem("zero_out")
        ln_chain, ln_ready = sem("ln_chain"), sem("ln_ready")
        xt_ready, xt_lo, xt_hi = sem("xt_ready"), sem("xt_lo"), sem("xt_hi")
        proj_ready, proj_read, v_ready, v_evac = sem("proj_ready"), sem("proj_read"), sem("v_ready"), sem("v_evac")
        res_ready, mid_ready = sem("res_ready"), sem("mid_ready")
        split_v, split_p, chain_v = sem("split_v"), sem("split_p"), sem("chain_v")
        parts_out = [sem("parts_out0"), sem("parts_out1")]
        v_out = [sem("v_out0"), sem("v_out1")]
        ring_ones = sem("ring_ones")
        q_in, k_in, va_in, vb_in = sem("q_in"), sem("k_in"), sem("va_in"), sem("vb_in")
        st_ready, exp_done, pv_done = sem("st_ready"), sem("exp_done"), sem("pv_done")
        s_ready, max_done, mx_ready = sem("s_ready"), sem("max_done"), sem("mx_ready")
        split_chain, msplit_ready = sem("split_chain"), sem("msplit_ready")
        mt_ready, mrow_ready = sem("mt_ready"), sem("mrow_ready")
        o_evac, o_turned, osum_ready = sem("o_evac"), sem("o_turned"), sem("osum_ready")
        rden_ready, rows_ready = sem("rden_ready"), sem("rows_ready")
        at_in = [sem("at_in0"), sem("at_in1")]
        at_tr, atT_copied, proj2_ready = sem("at_tr"), sem("atT_copied"), sem("proj2_ready")
        rows_out = sem("rows_out")
        x2_chain, xs_ready, xs_tr, xsT_copied = sem("x2_chain"), sem("xs_ready"), sem("xs_tr"), sem("xsT_copied")
        x_biased, a_out = sem("x_biased"), [sem("a_out0"), sem("a_out1")]
        gate_ready, gate_read = sem("gate_ready"), sem("gate_read")
        route_chain, exp_in, exp_out = sem("route_chain"), sem("gexp_in"), sem("gexp_out")
        rank_in, rank_out = sem("rank_in"), sem("rank_out")
        hot_s_ready, hot_v_ready, hot_p_ready = sem("hot_s_ready"), sem("hot_v_ready"), sem("hot_p_ready")
        slots_found, slots_ready = sem("slots_found"), sem("slots_ready")
        we_in = [sem("we_in0"), sem("we_in1")]
        xin_in = [sem("xin_in0"), sem("xin_in1")]
        xi_tr, xi_lo, xi_mid, xi_hi = sem("xi_tr"), sem("xi_lo"), sem("xi_mid"), sem("xi_hi")
        h_ready, h_act, h_dve = sem("h_ready"), sem("h_act"), sem("h_dve")
        y_ready, y_read, y_out = sem("y_ready"), sem("y_read"), [sem("y_out0"), sem("y_out1")]
        g_in = [sem(f"g_in{i}") for i in range(NT // 2)]
        o_chain, o_ready, out_done = sem("o_chain"), sem("o_ready"), sem("out_done")

        def lone_wait(eng):
            eng.sem_inc(waits_met, 1)

        def chain(eng, done, base):
            link = Chain(eng, done, base)

            def step(ins):
                link(ins)
                lone_wait(eng)
            return step

        var_ready, waits_met = sem("var_ready"), sem("waits_met")
        rstd_ready, dev_ready = sem("rstd_ready"), sem("dev_ready")
        block = ctx.enter_context(nc.Block())

        @block.sync
        def _(sp):
            for par in (0, 1):
                sp.sem_inc(parts_out[par], PARTS_STORED)
                sp.sem_inc(v_out[par], 16)
                sp.sem_inc(a_out[par], 16)
                sp.sem_inc(rows_out, 16)
            sp.dma_start(cst[:], consts).then_inc(const_in, 16)
            x_tiles = x[0].rearrange("(b t p) c -> b p t c", t=TPB, p=P)
            for b in range(NQ):
                sp.dma_start(x_t[:, TPB * b:TPB * b + TPB, :], x_tiles[b]).then_inc(x_in, 16)
                if b == 0:
                    sp.dma_start(wqkv[:].rearrange("p (k c) -> p k c", k=KC),
                                 w_qkv.rearrange("(k p) c -> p k c", p=P)).then_inc(w_in, 16)
                    sp.dma_start(bqk[:], b_qkv[0:2 * D].rearrange("(f p) -> p f", p=P),
                                 allow_slow_non_contiguous=True).then_inc(w_in, 16)
                    sp.dma_start(bv[:], b_qkv[2 * D:3 * D].partition_broadcast(P)).then_inc(w_in, 16)
                sp.wait_ge(x_in, 16 * (b + 1))
            sp.dma_start(wout[:].rearrange("p (k c) -> p k c", k=KC),
                         w_out.rearrange("(k p) c -> p k c", p=P)).then_inc(vec_in, 16)
            sp.dma_start(wgate[:].rearrange("p (k c) -> p k c", k=KC),
                         gate_w.rearrange("(k p) c -> p k c", p=P)).then_inc(vec_in, 16)
            sp.dma_start(bout[:], b_out.partition_broadcast(P)).then_inc(vec_in, 16)
            sp.dma_start(bgate[:], gate_b.partition_broadcast(P)).then_inc(vec_in, 16)
            def store_parts(c, par):
                for f in range(4):
                    if f < 2:
                        sp.wait_ge(split_v, 2 * c + f + 3)
                    else:
                        sp.wait_ge(split_p, 2 * c + f + 1)
                    sp.dma_start(qk_d[f // 2, :, (f % 2) * P:(f % 2) * P + P, ds(c * QW, QW)].rearrange("n p c -> p n c"),
                                 parts[par][:, f, :, :]).then_inc(parts_out[par], 16)

            def store_values(c, par):
                sp.wait_ge(v_evac, 2 * c + 4)
                sp.dma_start(v_d[:, :, ds(c * TPB * VW, TPB * VW)].rearrange("h p c -> p h c"),
                             vst[par].rearrange("p h t c -> p h (t c)")).then_inc(v_out[par], 16)

            def load_q(j):
                for b, part in enumerate(Q_PARTS):
                    sp.dma_start(q_ring[16 * b:16 * b + 16, ds((j % QRING) * QW, QW)],
                                 qk_d[0, part, ds(((j >> 3) % H) * HD, HD), ds((j % NQ) * QW, QW)]).then_inc(q_in, 16)

            def load_k(j):
                for b, part in enumerate(K_PARTS):
                    sp.dma_start(k_ring[16 * b:16 * b + 16, ds((j % KRING) * QW, QW)],
                                 qk_d[1, part, ds(((j >> 3) % H) * HD, HD), ds((j % NQ) * QW, QW)]).then_inc(k_in, 16)

            half = NT * VW // 2

            def load_v(head, second, done):
                o = half if second else 0
                sp.dma_start(v_sb[:, o:o + half], v_d[ds(head, 1), :, o:o + half].rearrange("h p c -> (h p) c")
                             ).then_inc(done, 16)

            def load_first_keys(c0, c1):
                for b, part in enumerate(K_PARTS):
                    sp.dma_start(k_ring[16 * b:16 * b + 16, c0 * QW:c1 * QW],
                                 qk_d[1, part, 0:HD, c0 * QW:c1 * QW]).then_inc(k_in, 16)

            with sp.Fori(0, NQ // 2 - 1) as i:
                for par in (0, 1):
                    store_parts(i * 2 + par, par)
                    store_values(i * 2 + par, par)
            for par in (0, 1):
                sp.wait_ge(parts_out[par], PARTS_STORED * (NQ // 2))
            sp.sem_inc(k_in, LOADED * (NQ - 2))
            load_first_keys(0, NQ - 2)
            store_parts(NQ - 2, 0)
            store_values(NQ - 2, 0)
            sp.wait_ge(parts_out[0], PARTS_STORED * (NQ // 2 + 1))
            sp.sem_inc(q_in, LOADED * (Q_AHEAD - 1))
            for b, part in enumerate(Q_PARTS):
                sp.dma_start(q_ring[16 * b:16 * b + 16, 0:Q_AHEAD * QW],
                             qk_d[0, part, 0:HD, 0:Q_AHEAD * QW]).then_inc(q_in, 16)
            store_parts(NQ - 1, 1)
            sp.wait_ge(parts_out[1], PARTS_STORED * (NQ // 2 + 1))
            load_first_keys(NQ - 2, NQ)
            store_values(NQ - 1, 1)
            for par in (0, 1):
                sp.wait_ge(v_out[par], 16 * (NQ // 2 + 1))
            load_v(0, False, va_in)
            sp.wait_ge(k_in, LOADED * NQ)
            sp.wait_ge(q_in, LOADED * Q_AHEAD)
            for j in range(NQ, K_AHEAD):
                load_k(j)

            def store_rows(it):
                sp.wait_ge(rows_ready, it + 1)
                lone_wait(sp)
                sp.wait_ge(rows_out, 16 * (it + 2))
                sp.dma_start(att_d[ds(it * QW, QW), :].rearrange("(t p) c -> p t c", p=P),
                             rows[:, ds((it % 2) * TPB * HD, TPB * HD)].rearrange("p (t c) -> p t c", c=HD)
                             ).then_inc(rows_out, 16)

            def attention_loads(it):
                sp.wait_ge(q_in, LOADED * (it + Q_AHEAD))
                lone_wait(sp)
                sp.wait_ge(k_in, LOADED * (it + K_AHEAD))
                lone_wait(sp)
                if not isinstance(it, int) or it > 0:
                    sp.wait_ge(st_ready, EXPS * it)
                    lone_wait(sp)
                load_q(it + Q_AHEAD)
                load_k(it + K_AHEAD)
                sp.wait_ge(pv_done, GROUPS * it + 2)
                load_v((it >> 3) % H, True, vb_in)
                sp.wait_ge(pv_done, GROUPS * it + GROUPS // 2 + 2)
                load_v(((it + 1) >> 3) % H, False, va_in)
                if not isinstance(it, int) or it > 0:
                    store_rows(it - 1)

            def load_expert(e, par):
                sp.dma_start(w1s[par], w1[ds(e, 1)].rearrange("e (k p) f -> p (e k) f", p=P)).then_inc(we_in[par], 16)
                sp.dma_start(w2s[par], w2[ds(e, 1)].rearrange("e (k p) c -> p (e k) c", p=P)).then_inc(we_in[par], 16)
                sp.dma_start(b1s[:, FT * par:FT * par + FT],
                             b1[ds(e, 1)].rearrange("e (f p) -> p (e f)", p=P),
                             allow_slow_non_contiguous=True).then_inc(we_in[par], 16)
                sp.dma_start(b2s[:, D * par:D * par + D],
                             b2[ds(e, 1)].rearrange("e c -> (e c)").partition_broadcast(P)).then_inc(we_in[par], 16)

            load_expert(0, 0)
            load_expert(1, 1)
            attention_loads(0)
            sp.wait_ge(zeros_ready, 1)
            for i in range(8):
                sp.dma_start(y_d[ds(i * T // 4, T // 4), :].rearrange("(p r) c -> p (r c)", p=P), zeros).then_inc(zero_out, 16)
            with sp.Fori(1, STEPS) as it:
                attention_loads(it)

            def load_rows(c, par):
                sp.wait_ge(at_tr, c + 1)
                sp.dma_start(at[par], att_d[ds(c * QW * D // HD, QW * D // HD), :].rearrange("(t p k) c -> p t (k c)", p=P, t=TPB)
                             ).then_inc(at_in[par], 16)

            def store_normed(c, par):
                sp.wait_ge(xs_ready, c + 1)
                lone_wait(sp)
                sp.dma_start(xn2_d[ds(c * QW, QW), :].rearrange("(t p) c -> p t c", p=P), xs[par]).then_inc(a_out[par], 16)

            sp.wait_ge(rows_out, 16 * STEPS)
            load_rows(0, 0)
            load_rows(1, 1)
            store_rows(STEPS - 1)
            sp.wait_ge(q_in, LOADED * (STEPS + Q_AHEAD))
            sp.wait_ge(k_in, LOADED * (STEPS + K_AHEAD))
            sp.wait_ge(va_in, 16 * (STEPS + 1))
            sp.wait_ge(rows_out, 16 * (STEPS + 2))
            with sp.Fori(0, NQ // 2 - 1) as i:
                for par in (0, 1):
                    store_normed(i * 2 + par, par)
                    load_rows(i * 2 + par + 2, par)
            store_normed(NQ - 2, 0)
            store_normed(NQ - 1, 1)

            with sp.Fori(0, E // 2 - 1) as i:
                for par in (0, 1):
                    sp.wait_ge(y_read, ST * (i * 2 + par + 1) + 2)
                    load_expert(i * 2 + par + 2, par)
            for par in (0, 1):
                sp.wait_ge(y_out[par], 16 * ST * (E // 2))
            for i in range(NT // 2):
                sp.dma_start(yg[i].rearrange("p t j c -> p (t j) c"),
                             y_d[4 * P * i:4 * P * i + 4 * P, :].rearrange("(r p) c -> p r c", p=P)).then_inc(g_in[i], 16)
            for i in range(NT // 2):
                sp.wait_ge(o_ready, 2 * i + 2)
                sp.dma_start(out[0, 2 * P * i:2 * P * i + 2 * P, :].rearrange("(t p) c -> p t c", p=P),
                             x_t[:, 2 * i:2 * i + 2, :]).then_inc(out_done, 16)
            sp.wait_ge(out_done, 16 * NT // 2)
            sp.wait_ge(zero_out, 16 * 8)

        @block.tensor
        def _(pe):
            mm, tr = nc.tensor.matmul, nc.tensor.transpose
            w3 = wqkv[:].rearrange("p (k c) -> p k c", k=KC)
            pe.sem_inc(pv_done, 2)
            pe.sem_inc(o_turned, 1)
            pe.sem_inc(at_tr, 2)
            pe.wait_ge(const_in, 16)

            def turn_chunk(c, par):
                pe.wait_ge(ln_ready, c + 1)
                pe.wait_ge(xt_lo, c + 1)
                pe.wait_ge(xt_hi, c + 1)
                for k in range(KC):
                    for t in range(TPB):
                        last = tr(bank(k)[:, t * P:t * P + P], xn[par][:, t, k * P:k * P + P], ident)
                    last.then_inc(xt_ready, 1)

            def project_features(c, par):
                pe.wait_ge(xt_lo, c + 2)
                pe.wait_ge(xt_hi, c + 2)
                for f in range(4):
                    pe.wait_ge(proj_read, 4 * c + f + 1)
                    for k in range(KC):
                        last = mm(bank(2 + f), w3[:, k, f * P:f * P + P], xnT[par][:, k, :], start=k == 0, stop=k == KC - 1)
                    last.then_inc(proj_ready, 1)

            def project_values(c, par):
                for b in range(2):
                    pe.wait_ge(v_evac, 2 * c + b + 1)
                    for t in (2 * b, 2 * b + 1):
                        for k in range(KC):
                            last = mm(bank(6 + b)[:, (t % 2) * D:(t % 2) * D + D], xnT[par][:, k, t * P:t * P + P],
                                      w3[:, k, 2 * D:3 * D], start=k == 0, stop=k == KC - 1)
                    last.then_inc(v_ready, 1)

            def project_chunk(c, par, more=True):
                project_features(c, par)
                if more:
                    turn_chunk(c + 1, 1 - par)
                project_values(c, par)

            turn_chunk(0, 0)
            pe.wait_ge(w_in, 48)
            with pe.Fori(0, NQ // 2 - 1) as i:
                for par in (0, 1):
                    project_chunk(i * 2 + par, par)
            project_chunk(NQ - 2, 0)
            project_chunk(NQ - 1, 1, more=False)

            def score_unit(u, base, qc, kc):
                pe.wait_ge(max_done, base + freed(u))
                qt, ch = u // NCH, u % NCH
                mm(bank(RING + u % RING), q_ring[0:NPR, ds(qc + qt * P, P)], k_ring[0:NPR, ds(kc + ch * QW, QW)],
                   start=True, stop=True).then_inc(s_ready, 1)

            def transpose_maxima(j):
                pe.wait_ge(msplit_ready, j + 1)
                for qt in range(TPB):
                    last = mm(ps[NPR:NAUG, 7 * QW + qt * P:7 * QW + qt * P + P], msplit[:, 4 * qt:4 * qt + 3], identb[:],
                              start=True, stop=True)
                last.then_inc(mt_ready, 1)

            pe.wait_ge(v_evac, 2 * NQ + 2)
            pe.wait_ge(proj_read, 4 * NQ + 4)
            pe.wait_ge(k_in, LOADED * NQ)
            pe.wait_ge(q_in, LOADED * Q_AHEAD)
            pe.wait_ge(consts_ready, 3)
            for j in (0, 1):
                for u in range(UNITS):
                    score_unit(u, UNITS * j, j * QW, 0)
                    if j == 1 and u == 12:
                        transpose_maxima(0)
            pe.wait_ge(ring_ones, 1)

            def pv_group(it, e0, g):
                pe.wait_ge(exp_done, e0 + (4 * g + 4 + RING))
                if g == 0:
                    pe.wait_ge(o_evac, it + 1)
                    pe.wait_ge(va_in, 16 * (it + 1))
                if g == GROUPS // 2:
                    pe.wait_ge(vb_in, 16 * (it + 1))
                for j in range(4):
                    kt = 4 * g + j
                    last = mm(ps[32 * j:32 * j + 32, 6 * QW:7 * QW], v_sb[:, kt * VW:kt * VW + VW],
                              p_ring[:, kt % 8, :],
                              start=g == 0, stop=g == GROUPS - 1)
                last.then_inc(pv_done, 1)

            def turn_outputs(it):
                pe.wait_ge(o_evac, it + 2)
                for qt in range(TPB):
                    last = tr(ps[:, 7 * QW + qt * P:7 * QW + qt * P + P], o_sb[:, qt * P:qt * P + P], ident)
                last.then_inc(o_turned, 1)

            def attention_pair(b, peeled=None):
                snap = pe.snap if peeled is None else (lambda v: v)
                qc, kc = snap((b % QRING) * QW), snap(((b >> 3) % 3) * T)
                qn, kn = snap(((b + 2) % QRING) * QW), snap((((b + 2) >> 3) % 3) * T)
                e0, u0 = snap(b * EXPS), snap((b + 2) * UNITS)
                for o in (0, 1):
                    attention_step(b + o, qc + o * QW, kc, qn + o * QW, kn, e0 + o * EXPS, u0 + o * UNITS,
                                   prev=peeled is None or b + o > 0, scores=peeled is None or b + o + 2 < STEPS,
                                   maxima=peeled is None or b + o + 1 < STEPS)

            def attention_step(it, qc, kc, qn, kn, e0, u0, prev, scores, maxima):
                if scores:
                    pe.wait_ge(q_in, LOADED * (it + 3))
                    pe.wait_ge(k_in, (((it + 2) >> 3) + 1) * (LOADED * NQ))

                def keys(kt):
                    pe.wait_ge(exp_done, e0 + freed(kt))
                    mm(bank(kt % RING), k_ring[0:NAUG, ds(kc + kt * P, P)], q_ring[0:NAUG, ds(qc, QW)],
                       start=True, stop=True).then_inc(st_ready, 1)

                def unit(u):
                    if scores:
                        score_unit(u, u0, qn, kn)

                for s in range(GROUPS):
                    if s >= PV_LAG:
                        pv_group(it, e0, s - PV_LAG)
                    elif prev:
                        pv_group(it - 1, e0 - EXPS, s - PV_LAG + GROUPS)
                    for j in range(3):
                        unit(4 * s + j)
                        if s == 0 and j == 0:
                            pe.wait_ge(mrow_ready, it + 1)
                        keys(4 * s + j)
                    if s == 3 and prev:
                        turn_outputs(it - 1)
                    if s == 5 and maxima:
                        if prev:
                            pe.wait_ge(osum_ready, it)
                        transpose_maxima(it + 1)
                    unit(4 * s + 3)
                    keys(4 * s + 3)

            attention_pair(0, peeled=True)
            with pe.Fori(1, STEPS // 2 - 1) as i:
                attention_pair(i * 2)
            attention_pair(STEPS - 2, peeled=True)
            for g in range(GROUPS - PV_LAG, GROUPS):
                pv_group(STEPS - 1, (STEPS - 1) * EXPS, g)

            wo3 = wout[:].rearrange("p (k c) -> p k c", k=KC)
            wg3 = wgate[:].rearrange("p (k c) -> p k c", k=KC)
            pe.wait_ge(vec_in, 64)

            def turn(c, i, par):
                pe.wait_ge(at_in[par], 16 * (i + 1))
                pe.wait_ge(atT_copied, c + 1)
                for k in range(KC):
                    for t in range(TPB):
                        last = tr(bank(k)[:, t * P:t * P + P], at[par][:, t, k * P:k * P + P], ident)
                last.then_inc(at_tr, 1)

            def project(c, par):
                pe.wait_ge(atT_copied, c + 2)
                pe.wait_ge(x2_chain, 2 * c + 2)
                for b in range(2):
                    for t in (2 * b, 2 * b + 1):
                        for k in range(KC):
                            last = mm(bank(2 + b)[:, (t % 2) * D:(t % 2) * D + D], atT[par][:, k * QW + t * P:k * QW + t * P + P],
                                      wo3[:, k, :], start=k == 0, stop=k == KC - 1)
                    last.then_inc(proj2_ready, 1)

            def turn_normed(c, par):
                pe.wait_ge(xs_ready, c + 1)
                pe.wait_ge(xsT_copied, c + 1)
                for k in range(KC):
                    for t in range(TPB):
                        last = tr(bank(4 + k)[:, t * P:t * P + P], xs[par][:, t, k * P:k * P + P], ident)
                last.then_inc(xs_tr, 1)

            def gate(c, par):
                pe.wait_ge(xsT_copied, c + 2)
                pe.wait_ge(gate_read, c + 1)
                for t in range(TPB):
                    for k in range(KC):
                        last = mm(bank(6)[:, t * E:t * E + E], xsT[par][:, k * QW + t * P:k * QW + t * P + P], wg3[:, k, :],
                                  start=k == 0, stop=k == KC - 1)
                last.then_inc(gate_ready, 1)

            def chunk_step(c, i, par, more=True):
                project(c, par)
                turn_normed(c - 1, 1 - par)
                if more:
                    turn(c + 1, i + par, 1 - par)
                gate(c - 1, 1 - par)

            turn(0, 0, 0)
            pe.wait_ge(osum_ready, STEPS - 1)
            turn_outputs(STEPS - 1)
            project(0, 0)
            turn(1, 0, 1)
            with pe.Fori(0, NQ // 2 - 1) as i:
                chunk_step(i * 2 + 1, i, 1)
                chunk_step(i * 2 + 2, i + 1, 0)
            chunk_step(NQ - 1, NQ // 2 - 1, 1, more=False)
            turn_normed(NQ - 1, 1)
            gate(NQ - 1, 1)

            pe.wait_ge(rank_in, 1)
            mm(bank(4)[:, 0:NT * E], trib[:], maskb, start=True, stop=True)
            mm(bank(5)[:, 0:NT * E], onesb[:], maskb, start=True, stop=True).then_inc(rank_out, 1)

            pe.wait_ge(hot_v_ready, 2)
            for n in range(NC):
                if n % 8 == 0:
                    pe.wait_ge(hot_p_ready, n // 8 + 1)
                last = mm(bank(6 + n // NT)[:, 0:2 * NS], hot_p[:, n, :], hot_v[:, n, :, :].rearrange("p v c -> p (v c)"),
                          start=n % NT == 0, stop=n % NT == NT - 1)
            last.then_inc(slots_found, 1)

            def turn_slots(e, i, par):
                pe.wait_ge(xin_in[par], 16 * ST * (i + 1))
                pe.wait_ge(xi_lo, e + 1)
                pe.wait_ge(xi_mid, e + 1)
                pe.wait_ge(xi_hi, e + 1)
                for k in range(KC):
                    for s in range(ST):
                        o = (k * ST + s) * P
                        last = tr(ps[:, o:o + P], xin[par][:, s, k * P:k * P + P], ident)
                last.then_inc(xi_tr, 1)

            def layer1(e, i, par, more):
                pe.wait_ge(we_in[par], 64 * (i + 1))
                pe.wait_ge(xi_lo, e + 2)
                pe.wait_ge(xi_mid, e + 2)
                pe.wait_ge(xi_hi, e + 2)
                for f in range(FT):
                    if f == FT - 1 and more:
                        pe.wait_ge(y_read, ST * e + 2)
                        turn_slots(e + 1, i + par, 1 - par)
                    done = h_act if f % 2 == 0 else h_dve
                    pe.wait_ge(done, FT // 2 * e + f // 2 + 1)
                    for hf in range(2):
                        for k in range(KC):
                            o = k * CAP + hf * CAP // 2
                            last = mm(bank(3 + 2 * (f % 2) + hf)[:, 0:CAP // 2], w1s[par][:, k, f * P:f * P + P],
                                      xinT[par][:, o:o + CAP // 2], start=k == 0, stop=k == KC - 1)
                    last.then_inc(h_ready, 1)

            def layer2(e, par):
                pe.wait_ge(h_act, FT // 2 * e + FT // 2 + 1)
                pe.wait_ge(h_dve, FT // 2 * e + FT // 2 + 1)
                for s in range(ST):
                    pe.wait_ge(y_read, ST * e + s + 1)
                    for f in range(FT):
                        last = mm(y_bank(e, par, s), hT[:, f, s * P:s * P + P], w2s[par][:, f, :],
                                  start=f == 0, stop=f == FT - 1)
                    last.then_inc(y_ready, 1)

            def y_bank(e, par, s):
                return bank(7)[:, 0:D] if (s + par) % 2 == 0 else bank(2)[:, D:2 * D]

            def expert(e, i, par, more):
                layer1(e, i, par, more)
                if more:
                    pe.wait_ge(xi_hi, e + 3)
                layer2(e, par)

            turn_slots(0, 0, 0)
            with pe.Fori(0, E // 2 - 1) as i:
                for par in (0, 1):
                    expert(i * 2 + par, i, par, True)
            expert(E - 2, E // 2 - 1, 0, True)
            expert(E - 1, E // 2 - 1, 1, False)

        @block.scalar
        def _(act):
            av = nc.scalar.activation
            act.sem_inc(xt_lo, 1)
            act.sem_inc(proj_read, 4)
            act.sem_inc(exp_done, RING)
            act.sem_inc(o_evac, 1)
            act.wait_ge(eps_ready, 1)

            def deviation(n, width):
                act.wait_ge(var_ready, n + 1)
                av(dev[:, 0:width], mv[:].rearrange("p (t s) -> p t s", s=2)[:, 0:width, 1], ACT.Sqrt,
                   bias=eps[:, 0:1]).then_inc(dev_ready, 1)

            def copy_turned(c, par):
                act.wait_ge(xt_ready, 2 * c + 1)
                av(xnT[par][:, 0, :], bank(0), ACT.Copy).then_inc(xt_lo, 1)

            def middle_part(c, par, f):
                act.wait_ge(res_ready, 2 * c + f - 1)
                av(parts[par][:, f, 1, :], res[:, 1, :], ACT.Copy).then_inc(mid_ready, 1)

            def project_chunk(c, i, par):
                act.wait_ge(parts_out[par], PARTS_STORED * (i + 1))
                for f in range(4):
                    act.wait_ge(proj_ready, 4 * c + f + 1)
                    if f < 2:
                        act.wait_ge(split_v, 2 * c + f + 1)
                    else:
                        act.wait_ge(split_p, 2 * c + f - 1)
                    scale = SCALE if f < 2 else 1.0
                    av(xf[:, f, :], bank(2 + f), ACT.Identity, bias=bqk[:, f:f + 1], scale=scale)
                    av(parts[par][:, f, 0, :], bank(2 + f), ACT.Identity, bias=bqk[:, f:f + 1],
                       scale=scale).then_inc(proj_read, 1)
                middle_part(c, par, 2)

            def chunk_step(c, i, par):
                deviation(c + 1, TPB)
                project_chunk(c, i, par)
                copy_turned(c + 1, 1 - par)
                middle_part(c, par, 3)

            deviation(0, TPB)
            copy_turned(0, 0)
            act.wait_ge(consts_ready, 3)
            with act.Fori(0, NQ // 2 - 1) as i:
                for par in (0, 1):
                    chunk_step(i * 2 + par, i, par)
            chunk_step(NQ - 2, NQ // 2 - 1, 0)
            project_chunk(NQ - 1, NQ // 2 - 1, 1)
            middle_part(NQ - 1, 1, 3)

            def copy_maxima(j):
                act.wait_ge(mt_ready, j + 1)
                av(q_ring[NPR:NAUG, ds((j % QRING) * QW, QW)], ps[NPR:NAUG, 7 * QW:8 * QW], ACT.Copy).then_inc(mrow_ready, 1)

            for par in (0, 1):
                act.wait_ge(parts_out[par], PARTS_STORED * (NQ // 2 + 1))
            copy_maxima(0)

            def evacuate(it):
                act.wait_ge(pv_done, GROUPS * it + GROUPS + 2)
                act.wait_ge(o_turned, it + 1)
                av(o_sb[:], bank(6), ACT.Copy).then_inc(o_evac, 1)

            def attention_step(it, prev=True, maxima=True):
                snap = (lambda v: v) if isinstance(it, int) else act.snap
                e0, g0 = snap(it * EXPS), snap(it * GROUPS)
                for n in range(EXPS):
                    act.wait_ge(st_ready, e0 + n + 1)
                    act.wait_ge(pv_done, g0 + n // 4 + 1)
                    av(p_ring[:, n % 8, :], bank(n % RING), ACT.Exp).then_inc(exp_done, 1)
                    if n == 4 * (PV_LAG - 1) - 1 and prev:
                        evacuate(it - 1)
                    if n == 25 and maxima:
                        copy_maxima(it + 1)

            attention_step(0, prev=False)
            with act.Fori(1, STEPS - 1) as it:
                attention_step(it)
            attention_step(STEPS - 1, maxima=False)
            evacuate(STEPS - 1)

            def copy_rows(c, par):
                act.wait_ge(at_tr, c + 3)
                av(atT[par], bank(0, 2), ACT.Copy).then_inc(atT_copied, 1)

            def copy_normed(c, par):
                act.wait_ge(xs_tr, c + 1)
                av(xsT[par], bank(4, 2), ACT.Copy).then_inc(xsT_copied, 1)

            def chunk_copies(c, par, more=True):
                copy_normed(c - 1, 1 - par)
                if more:
                    copy_rows(c + 1, 1 - par)
                deviation(NQ + c, TPB)

            act.wait_ge(q_in, LOADED * (STEPS + Q_AHEAD))
            act.wait_ge(k_in, LOADED * (STEPS + K_AHEAD))
            act.sem_inc(atT_copied, 1)
            act.sem_inc(xsT_copied, 1)
            copy_rows(0, 0)
            copy_rows(1, 1)
            deviation(NQ, TPB)
            with act.Fori(0, NQ // 2 - 1) as i:
                chunk_copies(i * 2 + 1, 1)
                chunk_copies(i * 2 + 2, 0)
            chunk_copies(NQ - 1, 1, more=False)
            copy_normed(NQ - 1, 1)

            act.wait_ge(exp_in, 1)
            av(rt[2], rt[1], ACT.Exp).then_inc(exp_out, 1)

            act.wait_ge(hot_s_ready, 1)
            av(hot_v[:, :, 1, :], hot_s, ACT.Copy, scale=row_n).then_inc(hot_v_ready, 1)

            act.sem_inc(xi_lo, 1)
            act.sem_inc(h_act, 1)

            def slots_copy(e, par):
                act.wait_ge(xi_tr, e + 1)
                av(xinT[par][:, 0:QW], bank(0), ACT.Copy).then_inc(xi_lo, 1)

            def expert(e, i, par, more):
                act.wait_ge(we_in[par], 64 * (i + 1))
                for f in range(0, FT, 2):
                    act.wait_ge(h_ready, FT * e + f + 1)
                    av(hT[:, f, :].rearrange("p (a c) -> p a c", a=2),
                       bank(3, 2).rearrange("p (a c) -> p a c", a=2)[:, :, 0:CAP // 2], ACT.Relu,
                       bias=b1s[:, FT * par + f:FT * par + f + 1]).then_inc(h_act, 1)
                if more:
                    slots_copy(e + 1, 1 - par)

            slots_copy(0, 0)
            with act.Fori(0, E // 2 - 1) as i:
                for par in (0, 1):
                    expert(i * 2 + par, i, par, True)
            expert(E - 2, E // 2 - 1, 0, True)
            expert(E - 1, E // 2 - 1, 1, False)

        @block.gpsimd
        def _(pool):
            g = nc.gpsimd
            pool.sem_inc(split_p, 2)
            g.memset(zeros, 0.0).then_inc(zeros_ready, 1)
            for par in (0, 1):
                g.memset(vst[par][:, :, :, HD:VW], 0.0).then_inc(vst_ready, 1)
                pool.wait_ge(vst_ready, 2 * par + 1)
                g.memset(vst[par][:, :, :, HD:HD + 1], 1.0).then_inc(vst_ready, 1)
            pool.wait_ge(vst_ready, 4)
            g.memset(k_ring[NPR:NAUG, :], 1.0).then_inc(ring_ones, 1)

            pool.wait_ge(ring_ones, 1)

            def split_chunk(c, par):
                for f in (2, 3):
                    pool.wait_ge(proj_read, 4 * c + f + 5)
                    g.tensor_tensor(res[:, 1, :], xf[:, f, :], parts[par][:, f, 0, :], ALU.subtract).then_inc(res_ready, 1)
                    pool.wait_ge(mid_ready, 2 * c + f - 1)
                    g.tensor_tensor(parts[par][:, f, 2, :], res[:, 1, :], parts[par][:, f, 1, :],
                                    ALU.subtract).then_inc(split_p, 1)
                    pool.wait_ge(split_p, 2 * c + f + 1)

            with pool.Fori(0, NQ // 2) as i:
                for par in (0, 1):
                    split_chunk(i * 2 + par, par)

            msp = msplit[:].rearrange("p (t n) -> p n t", n=4)

            def split_maxima(j):
                link = chain(pool, split_chain, j * 4)
                pool.wait_ge(mx_ready, j + 1)
                if not isinstance(j, int) or j > 0:
                    pool.wait_ge(mt_ready, j)
                lone_wait(pool)
                link(g.tensor_scalar(mneg[:], mx[:], -1.0, None, ALU.mult))
                link(g.tensor_copy(msp[:, 0, :], mneg[:]))
                link(g.tensor_tensor(mres[:], mneg[:], msp[:, 0, :], ALU.subtract))
                link(g.tensor_copy(msp[:, 1, :], mres[:]))
                g.tensor_tensor(msp[:, 2, :], mres[:], msp[:, 1, :], ALU.subtract).then_inc(msplit_ready, 1)

            split_maxima(0)
            pool.wait_ge(vec_in, 64)
            pool.wait_ge(ln_ready, NQ)
            with pool.Fori(0, NQ) as c:
                four = x_all[:, ds(c * TPB * D, TPB * D)].rearrange("p (t c) -> p t c", t=TPB)
                g.tensor_tensor(four, four, bout[:].unsqueeze(1).to_broadcast([P, TPB, D]), ALU.add).then_inc(x_biased, 1)
            with pool.Fori(1, STEPS) as j:
                split_maxima(j)

            pool.wait_ge(hot_s_ready, 1)
            g.tensor_tensor(hot_v[:, :, 0, :], hot_s, tile_n.unsqueeze(2).to_broadcast([P, NC, NS]),
                            ALU.mult).then_inc(hot_v_ready, 1)

            def gather(e):
                for s in range(ST):
                    g.indirect_dma_start(xin[e % 2][:, s, :], None, xn2_d,
                                         bass.IndirectOffsetOnAxis(slot_src[:, ST * e + s:ST * e + s + 1], 0)
                                         ).then_inc(xin_in[e % 2], 16)

            def scatter(e):
                for s in range(ST):
                    pool.wait_ge(y_read, ST * e + s + 3)
                    g.indirect_dma_start(y_d, bass.IndirectOffsetOnAxis(slot_dst[:, ST * e + s:ST * e + s + 1], 0),
                                         ys[e % 2][:, s, :], None, bounds_check=2 * T - 1, oob_is_err=False
                                         ).then_inc(y_out[e % 2], 16)

            pool.wait_ge(zero_out, 16 * 8)
            for par in (0, 1):
                pool.wait_ge(a_out[par], 16 * (NQ // 2 + 1))
            pool.wait_ge(slots_ready, 1)
            gather(0)
            gather(1)
            for e in range(E):
                if e + 2 < E:
                    pool.wait_ge(xi_tr, e + 1)
                    gather(e + 2)
                scatter(e)

        @block.vector
        def _(dve):
            v = nc.vector
            dve.sem_inc(xt_hi, 1)
            dve.sem_inc(v_evac, 2)
            dve.sem_inc(split_v, 2)
            dve.sem_inc(max_done, RING)
            v.memset(eps[:], EPS).then_inc(eps_ready, 1)

            st3 = stats[:].rearrange("p (t s) -> p t s", s=6)
            mv3 = mv[:].rearrange("p (t s) -> p t s", s=2)

            def normalise(c, par):
                link = chain(dve, ln_chain, c * 1)
                dve.wait_ge(x_in, 16 * (c + 1))
                lone_wait(dve)
                for t in range(TPB):
                    last = v.bn_stats(st3[:, t, :], x_all[:, ds((c * TPB + t) * D, D)])
                link(last)
                for t in range(TPB):
                    last = v.bn_aggr(mv3[:, t, :], st3[:, t, :])
                last.then_inc(var_ready, 1)
                dve.wait_ge(dev_ready, c + 1)
                v.reciprocal(rstd[:], dev[:]).then_inc(rstd_ready, 1)
                dve.wait_ge(rstd_ready, c + 1)
                for t in range(TPB):
                    last = v.tensor_scalar(xn[par][:, t, :], x_all[:, ds((c * TPB + t) * D, D)], mv3[:, t, 0:1],
                                           rstd[:, t:t + 1], ALU.subtract, ALU.mult)
                last.then_inc(ln_ready, 1)

            def copy_turned(c, par):
                dve.wait_ge(xt_ready, 2 * c + 2)
                v.tensor_copy(xnT[par][:, 1, :], bank(1)).then_inc(xt_hi, 1)

            def split_queries(c, par):
                link = Chain(dve, chain_v, c * 4)
                for f in (0, 1):
                    dve.wait_ge(proj_read, 4 * c + f + 5)
                    link(v.tensor_tensor(res[:, 0, :], xf[:, f, :], parts[par][:, f, 0, :], ALU.subtract))
                    link(v.tensor_copy(parts[par][:, f, 1, :], res[:, 0, :]))
                    v.tensor_tensor(parts[par][:, f, 2, :], res[:, 0, :], parts[par][:, f, 1, :],
                                    ALU.subtract).then_inc(split_v, 1)
                    dve.wait_ge(split_v, 2 * c + f + 3)

            def take_values(c, i, par):
                dve.wait_ge(v_out[par], 16 * (i + 1))
                for b in range(2):
                    dve.wait_ge(v_ready, 2 * c + b + 1)
                    for t in range(2):
                        last = v.tensor_tensor(vst[par][:, :, 2 * b + t, 0:HD],
                                               bank(6 + b)[:, t * D:t * D + D].rearrange("p (h c) -> p h c", h=H),
                                               bv[:].rearrange("p (h c) -> p h c", h=H), ALU.add)
                    last.then_inc(v_evac, 1)

            def chunk_step(c, i, par, more=True):
                if more:
                    normalise(c + 1, 1 - par)
                split_queries(c, par)
                if more:
                    copy_turned(c + 1, 1 - par)
                take_values(c, i, par)

            normalise(0, 0)
            dve.wait_ge(const_in, 16)
            dve.wait_ge(w_in, 48)
            v.tensor_scalar(bqk[:, 0:2], bqk[:, 0:2], SCALE, None, ALU.mult).then_inc(consts_ready, 1)
            v.tensor_copy(identb[:], ident)
            v.tensor_copy(trib[:], cst[:, P:2 * P]).then_inc(consts_ready, 1)
            v.memset(onesb[:], 1.0).then_inc(consts_ready, 1)
            dve.wait_ge(vst_ready, 4)
            copy_turned(0, 0)
            with dve.Fori(0, NQ // 2 - 1) as i:
                for par in (0, 1):
                    chunk_step(i * 2 + par, i, par)
            chunk_step(NQ - 2, NQ // 2 - 1, 0)
            chunk_step(NQ - 1, NQ // 2 - 1, 1, more=False)

            groups = bank(7).rearrange("p (t g c) -> p t c g", t=TPB, g=4)[:, :, 0:HD + 1, :]
            sums = osum[:].rearrange("p (t c) -> p t c", t=TPB)

            def maximum(u, base, par):
                dve.wait_ge(s_ready, base + u + 1)
                v.tensor_reduce(mpart[:, UNITS * par + u:UNITS * par + u + 1], bank(RING + u % RING), AX.X,
                                ALU.max).then_inc(max_done, 1)

            def reduce_maxima(j, par):
                dve.wait_ge(max_done, (j + 1) * UNITS + RING)
                if not isinstance(j, int) or j > 0:
                    dve.wait_ge(msplit_ready, j)
                v.tensor_reduce(mx[:], mpart[:, UNITS * par:UNITS * par + UNITS].rearrange("p (t c) -> p t c", t=TPB),
                                AX.X, ALU.max).then_inc(mx_ready, 1)

            def sum_groups(it):
                if not isinstance(it, int) or it > 0:
                    dve.wait_ge(rows_ready, it)
                dve.wait_ge(o_turned, it + 2)
                v.tensor_reduce(sums, groups, AX.X, ALU.add).then_inc(osum_ready, 1)

            def invert_sums(it):
                dve.wait_ge(osum_ready, it + 1)
                v.reciprocal(rden[:], sums[:, :, HD]).then_inc(rden_ready, 1)

            def write_rows(it):
                dve.wait_ge(rows_out, 16 * (it + 1))
                dve.wait_ge(rden_ready, it + 1)
                v.tensor_tensor(rows[:, ds((it % 2) * TPB * HD, TPB * HD)].rearrange("p (t c) -> p t c", c=HD),
                                sums[:, :, 0:HD], rden[:].unsqueeze(2).to_broadcast([P, TPB, HD]),
                                ALU.mult).then_inc(rows_ready, 1)

            for j in (0, 1):
                for u in range(UNITS):
                    maximum(u, UNITS * j, j)
                    if u == 1 and j == 1:
                        reduce_maxima(0, 0)

            def attention_step(it, par, u0, prev=True, scores=True, maxima=True):
                dve.wait_ge(mx_ready, it + 1)
                for u in range(UNITS):
                    if scores:
                        maximum(u, u0, par)
                    if u == 1 and maxima:
                        reduce_maxima(it + 1, 1 - par)
                    if prev:
                        if u == 17:
                            sum_groups(it - 1)
                        if u == 18:
                            invert_sums(it - 1)
                        if u == 19:
                            write_rows(it - 1)

            attention_step(0, 0, 2 * UNITS, prev=False)
            attention_step(1, 1, 3 * UNITS)
            with dve.Fori(1, STEPS // 2 - 1) as i:
                u0 = dve.snap((i * 2 + 2) * UNITS)
                for o in (0, 1):
                    attention_step(i * 2 + o, o, u0 + o * UNITS)
            attention_step(STEPS - 2, 0, 0, scores=False)
            attention_step(STEPS - 1, 1, 0, scores=False, maxima=False)
            sum_groups(STEPS - 1)
            invert_sums(STEPS - 1)
            write_rows(STEPS - 1)

            dve.wait_ge(vec_in, 64)
            dve.wait_ge(x_biased, NQ)
            dve.sem_inc(x2_chain, 2)
            logits = rt[0]

            def residual(c, i, par):
                for b in range(2):
                    dve.wait_ge(proj2_ready, 2 * c + b + 1)
                    two = x_all[:, ds((c * TPB + 2 * b) * D, 2 * D)]
                    v.tensor_tensor(two, bank(2 + b), two, ALU.add).then_inc(x2_chain, 1)
                link = chain(dve, ln_chain, c + NQ)
                dve.wait_ge(x2_chain, 2 * c + 4)
                lone_wait(dve)
                for t in range(TPB):
                    last = v.bn_stats(st3[:, t, :], x_all[:, ds((c * TPB + t) * D, D)])
                link(last)
                for t in range(TPB):
                    last = v.bn_aggr(mv3[:, t, :], st3[:, t, :])
                last.then_inc(var_ready, 1)
                dve.wait_ge(dev_ready, NQ + c + 1)
                v.reciprocal(rstd[:], dev[:]).then_inc(rstd_ready, 1)
                dve.wait_ge(a_out[par], 16 * (i + 1))
                dve.wait_ge(rstd_ready, NQ + c + 1)
                for t in range(TPB):
                    last = v.tensor_scalar(xs[par][:, t, :], x_all[:, ds((c * TPB + t) * D, D)], mv3[:, t, 0:1],
                                           rstd[:, t:t + 1], ALU.subtract, ALU.mult)
                last.then_inc(xs_ready, 1)

            def read_gate(c):
                dve.wait_ge(gate_ready, c + 1)
                v.tensor_tensor(arena[:, ds(c * TPB * E, TPB * E)].rearrange("p (t e) -> p t e", e=E),
                                bank(6)[:, 0:TPB * E].rearrange("p (t e) -> p t e", e=E),
                                bgate[:].unsqueeze(1).to_broadcast([P, TPB, E]), ALU.add).then_inc(gate_read, 1)

            dve.sem_inc(gate_read, 1)
            dve.wait_ge(q_in, LOADED * (STEPS + Q_AHEAD))
            dve.wait_ge(k_in, LOADED * (STEPS + K_AHEAD))
            residual(0, 0, 0)
            with dve.Fori(0, NQ // 2 - 1) as i:
                for par in (1, 0):
                    c = i * 2 + (1 if par else 2)
                    residual(c, i if par else i + 1, par)
                    read_gate(c - 1)
            residual(NQ - 1, NQ // 2 - 1, 1)
            read_gate(NQ - 2)
            read_gate(NQ - 1)
            dve.wait_ge(gate_read, NQ + 1)

            link = Chain(dve, route_chain)

            def wide(a):
                return a.unsqueeze(2).to_broadcast([P, NT, E])

            ex = iota_e.unsqueeze(1).to_broadcast([P, NT, E])
            rmax, rsum, rrec = r1[0], r1[1], r1[2]
            link(v.tensor_reduce(rmax, logits, AX.X, ALU.max))
            v.tensor_tensor(rt[1], logits, wide(rmax), ALU.subtract).then_inc(exp_in, 1)
            dve.wait_ge(exp_out, 1)
            link(v.tensor_reduce(rsum, rt[2], AX.X, ALU.add))
            link(v.reciprocal(rrec, rsum))
            link(v.tensor_tensor(rt[3], rt[2], wide(rrec), ALU.mult))
            prob = rt[3]
            sel = []
            for n in range(2):
                top, idx = r1[3 + n], r1[5 + n]
                link(v.tensor_reduce(top, prob, AX.X, ALU.max))
                link(v.tensor_tensor(rt[4], prob, wide(top), ALU.is_lt))
                link(v.scalar_tensor_tensor(rt[5], rt[4], float(E), ex, ALU.mult, ALU.add))
                link(v.tensor_reduce(idx, rt[5], AX.X, ALU.min))
                pick = rt[6 + n]
                link(v.tensor_tensor(pick, ex, wide(idx), ALU.is_equal))
                sel.append(pick)
                if n == 0:
                    link(v.scalar_tensor_tensor(rt[8], pick, -2.0, prob, ALU.mult, ALU.add))
                    prob = rt[8]
            v.tensor_tensor(maskb.rearrange("p (t e) -> p t e", e=E), sel[0], sel[1], ALU.add).then_inc(rank_in, 1)
            dve.wait_ge(rank_out, 1)
            tot = [rt[9], rt[10]]
            link(v.tensor_copy(tot[0], bank(5)[:, 0:NT * E].rearrange("p (t e) -> p t e", e=E)))
            cur, step = 0, 1
            while step < NT:
                a, b = tot[cur], tot[1 - cur]
                link(v.tensor_copy(b[:, 0:step, :], a[:, 0:step, :]))
                link(v.tensor_tensor(b[:, step:NT, :], a[:, step:NT, :], a[:, 0:NT - step, :], ALU.add))
                cur, step = 1 - cur, 2 * step
            rank, slot = rt[11], rt[12]
            link(v.tensor_copy(rank, bank(4)[:, 0:NT * E].rearrange("p (t e) -> p t e", e=E)))
            link(v.tensor_tensor(rank[:, 1:NT, :], rank[:, 1:NT, :], tot[cur][:, 0:NT - 1, :], ALU.add))
            over = rt[13]
            link(v.tensor_scalar(over, rank, float(CAP), None, ALU.is_gt))
            link(v.tensor_tensor(slot, rank, slot_base.unsqueeze(1).to_broadcast([P, NT, E]), ALU.add))
            den = r1[7]
            link(v.tensor_tensor(den, r1[3], r1[4], ALU.add))
            link(v.reciprocal(den, den))
            for n in range(2):
                s_n, o_n, f_n = r1[8 + n], r1[10 + n], r1[12 + n]
                link(v.tensor_tensor(rt[14], sel[n], slot, ALU.mult))
                link(v.tensor_reduce(s_n, rt[14], AX.X, ALU.add))
                link(v.tensor_tensor(rt[15], sel[n], over, ALU.mult))
                link(v.tensor_reduce(o_n, rt[15], AX.X, ALU.add))
                link(v.scalar_tensor_tensor(gslot[:, n * NT:n * NT + NT], o_n, BIG, s_n, ALU.mult, ALU.add))
                link(v.tensor_scalar(o_n, o_n, -1.0, 1.0, ALU.mult, ALU.add))
                link(v.tensor_tensor(f_n, r1[3 + n], den, ALU.mult))
                link(v.tensor_tensor(wgt[:, n * NT:n * NT + NT], f_n, o_n, ALU.mult))
            link(v.tensor_copy(gint, gslot))
            link(v.tensor_scalar(gint, gint, P.bit_length() - 1, None, ALU.logical_shift_right))
            link(v.tensor_copy(gtile, gint))
            link(v.scalar_tensor_tensor(gcol, gtile, -float(P), gslot, ALU.mult, ALU.add))
            v.tensor_tensor(hot_s, iota_s.unsqueeze(1).to_broadcast([P, NC, NS]),
                            gtile.unsqueeze(2).to_broadcast([P, NC, NS]), ALU.is_equal).then_inc(hot_s_ready, 1)
            for n in range(0, NC, 8):
                v.tensor_tensor(hot_p[:, n:n + 8, :], iota_p.unsqueeze(1).to_broadcast([P, 8, P]),
                                gcol[:, n:n + 8].unsqueeze(2).to_broadcast([P, 8, P]), ALU.is_equal).then_inc(hot_p_ready, 1)
            dve.wait_ge(slots_found, 1)
            first, both, second, none, row, src, dst = dec[0:7]
            link(v.tensor_copy(first, bank(6)[:, 0:2 * NS]))
            link(v.tensor_tensor(both, bank(7)[:, 0:2 * NS], first, ALU.add))
            link(v.tensor_scalar(second[:, 0:NS], bank(7)[:, NS:2 * NS], 0.0, None, ALU.is_gt))
            link(v.tensor_scalar(none[:, 0:NS], both[:, NS:2 * NS], 0.0, None, ALU.is_equal))
            link(v.tensor_scalar(row[:, 0:NS], both[:, NS:2 * NS], 1.0, None, ALU.subtract))
            link(v.scalar_tensor_tensor(src[:, 0:NS], both[:, 0:NS], float(P), row[:, 0:NS], ALU.mult, ALU.add))
            link(v.tensor_scalar(slot_src[:], src[:, 0:NS], 0.0, None, ALU.max))
            link(v.scalar_tensor_tensor(dst[:, 0:NS], both[:, 0:NS], 2.0, second[:, 0:NS], ALU.mult, ALU.add))
            link(v.scalar_tensor_tensor(dst[:, 0:NS], dst[:, 0:NS], float(P), row[:, 0:NS], ALU.mult, ALU.add))
            link(v.scalar_tensor_tensor(dst[:, 0:NS], none[:, 0:NS], BIG, dst[:, 0:NS], ALU.mult, ALU.add))
            v.tensor_copy(slot_dst[:], dst[:, 0:NS]).then_inc(slots_ready, 1)

            dve.sem_inc(xi_mid, 1)
            dve.sem_inc(xi_hi, 1)
            dve.sem_inc(h_dve, 1)
            dve.sem_inc(y_read, 2)

            def slots_copy(e, par):
                dve.wait_ge(xi_tr, e + 1)
                v.tensor_copy(xinT[par][:, QW:2 * QW], bank(1)).then_inc(xi_mid, 1)
                v.tensor_copy(xinT[par][:, 2 * QW:2 * CAP], bank(2)[:, 0:2 * CAP - 2 * QW]).then_inc(xi_hi, 1)

            def expert(e, i, par, more):
                dve.wait_ge(we_in[par], 64 * (i + 1))
                for f in range(1, FT, 2):
                    if f == FT - 1 and more:
                        slots_copy(e + 1, 1 - par)
                    dve.wait_ge(h_ready, FT * e + f + 1)
                    v.tensor_scalar(hT[:, f, :].rearrange("p (a c) -> p a c", a=2),
                                    bank(5, 2).rearrange("p (a c) -> p a c", a=2)[:, :, 0:CAP // 2],
                                    b1s[:, FT * par + f:FT * par + f + 1], 0.0, ALU.add, ALU.max).then_inc(h_dve, 1)
                if not isinstance(i, int) or i > 0:
                    dve.wait_ge(y_out[par], 16 * ST * i)
                for s in range(ST):
                    src = bank(7)[:, 0:D] if (s + par) % 2 == 0 else bank(2)[:, D:2 * D]
                    dve.wait_ge(y_ready, ST * e + s + 1)
                    v.tensor_tensor(ys[par][:, s, :], src, b2s[:, D * par:D * par + D], ALU.add).then_inc(y_read, 1)

            slots_copy(0, 0)
            expert(0, 0, 0, True)
            expert(1, 0, 1, True)
            with dve.Fori(1, E // 2 - 1) as i:
                for par in (0, 1):
                    expert(i * 2 + par, i, par, True)
            expert(E - 2, E // 2 - 1, 0, True)
            expert(E - 1, E // 2 - 1, 1, False)

            for t in range(NT):
                if t % 2 == 0:
                    dve.wait_ge(g_in[t // 2], 16)
                for j in range(2):
                    if j == 1:
                        dve.wait_ge(o_chain, t + 1)
                    v.scalar_tensor_tensor(x_t[:, t, :], yg[t // 2][:, t % 2, j, :], wgt[:, j * NT + t:j * NT + t + 1],
                                           x_t[:, t, :], ALU.mult, ALU.add).then_inc((o_chain, o_ready)[j], 1)


INPUTS = ["L0_attn_x", "L0_attn_W_qkv", "L0_attn_b_qkv", "L0_attn_W_out", "L0_attn_b_out", "L0_ffn_gate_w",
          "L0_ffn_gate_b", "L0_ffn_w1", "L0_ffn_b1", "L0_ffn_w2", "L0_ffn_b2"]


def constants():
    c = np.zeros((P, CW), np.float32)
    c[:, 0:P] = np.eye(P)
    c[:, P:2 * P] = np.triu(np.ones((P, P)))
    c[:, 2 * P:2 * P + E] = np.arange(E)
    c[:, 2 * P + E:2 * P + 2 * E] = np.arange(E) * CAP - 1
    o = 2 * P + 2 * E
    c[:, o:o + P] = np.arange(P)
    c[:, o + P:o + P + NS] = np.arange(NS)
    c[:, o + P + NS:CW - 1] = np.arange(NC) % NT
    c[:, CW - 1] = np.arange(P) + 1
    return c


def kernel(**inputs):
    import concourse.bacc as bacc
    from concourse.bass_utils import run_bass_kernel_spmd

    nc = bacc.Bacc("TRN2", target_bir_lowering=False, num_devices=1)
    arrays = {name: np.ascontiguousarray(inputs[name]) for name in INPUTS}
    arrays["consts"] = constants()
    aps = [nc.dram_tensor(n, a.shape, mybir.dt.from_np(a.dtype), kind="ExternalInput").ap() for n, a in arrays.items()]
    out = nc.dram_tensor("out", (1, T, D), F32, kind="ExternalOutput").ap()
    build(nc, *aps, out)
    r = run_bass_kernel_spmd(nc, [arrays], core_ids=[0])
    return r.results[0]["out"]
```
